# Optimizing a Trainium2 kernel written in Bass

```python
import numpy as np
import jax
import jax.numpy as jnp

def _softmax(x, axis=-1):
    return jax.nn.softmax(x, axis=axis)

def _gelu(x):
    return jax.nn.gelu(x, approximate=True)

def _silu(x):
    return jax.nn.silu(x)

def _sigmoid(x):
    return jax.nn.sigmoid(x)

def _layernorm(x, axis=-1, eps=1e-05):
    m = jnp.mean(x, axis=axis, keepdims=True)
    v = jnp.var(x, axis=axis, keepdims=True)
    return (x - m) / jnp.sqrt(v + eps)

def _scatter_add(tgt, idx, src, axis=0):
    return tgt.at[idx].add(src)

def _segment_sum(src, seg, n):
    return jax.ops.segment_sum(src, seg, n)
kernel_name = 'mk_gnn_preln_d2_gnn_r8_32da44'

def setup_inputs(seed: int=0):
    np.random.seed(seed)
    _w = jnp.asarray

    def _rec_inputs():
        import jax
        import jax.numpy as jnp
        _gk = jax.random.key(seed)
        x = -0.000202 + 1 * jax.random.normal(jax.random.fold_in(_gk, 1), (6250, 64), jnp.float32)
        src = jax.random.randint(jax.random.fold_in(_gk, 2), (200000,), 0, 6250, jnp.int32)
        dst = jax.random.randint(jax.random.fold_in(_gk, 3), (200000,), 0, 6250, jnp.int32)
        _o = jnp.argsort(dst, stable=True)
        src = src[_o]
        dst = dst[_o]
        edge_attr_64 = -8.16379e-05 + 0.999858 * jax.random.normal(jax.random.fold_in(_gk, 12), (200000, 64), jnp.float32)
        return (x, src, dst, edge_attr_64)
    x, src, dst, edge_attr_64 = _rec_inputs()

    def _L0_gnn_setup():
        import jax, jax.numpy as jnp
        import numpy as np
        N_NODES = 12500
        N_EDGES = 150000
        D = 64
        key = jax.random.key(seed)
        k1, k2, k3 = jax.random.split(key, 3)
        x = jax.random.normal(k1, (N_NODES, D), dtype=jnp.float32)
        edge_index = jax.random.randint(k2, (2, N_EDGES), 0, N_NODES, dtype=jnp.int64)
        W = jax.random.normal(k3, (D, D), dtype=jnp.float32) / np.sqrt(D)
        b = jnp.zeros((D,), dtype=jnp.float32)
        return {'x': x, 'edge_index': edge_index, 'W': W, 'b': b}
    _L0_gnn_all = _L0_gnn_setup()
    _L0_gnn_in = {k: v for k, v in _L0_gnn_all.items() if k in ('W', 'b')}
    del _L0_gnn_all

    def _L1_gnn_setup():
        import jax, jax.numpy as jnp
        import numpy as np
        N_NODES = 12500
        N_EDGES = 200000
        D = 64

        def _mlp(x, W1, b1, W2, b2):
            return jnp.dot(jax.nn.relu(jnp.dot(x, W1) + b1), W2) + b2
        key = jax.random.key(seed)
        ks = jax.random.split(key, 12)
        s = lambda fan_in: 1.0 / np.sqrt(fan_in)
        return {'node_x': jax.random.normal(ks[0], (N_NODES, D), jnp.float32), 'edge_x': jax.random.normal(ks[1], (N_EDGES, D), jnp.float32), 'sources': jax.random.randint(ks[2], (N_EDGES,), 0, N_NODES), 'targets': jax.random.randint(ks[3], (N_EDGES,), 0, N_NODES), 'msg_W1': jax.random.normal(ks[4], (3 * D, D), jnp.float32) * s(3 * D), 'msg_b1': jnp.zeros((D,), jnp.float32), 'msg_W2': jax.random.normal(ks[5], (D, D), jnp.float32) * s(D), 'msg_b2': jnp.zeros((D,), jnp.float32), 'upd_W1': jax.random.normal(ks[6], (2 * D, D), jnp.float32) * s(2 * D), 'upd_b1': jnp.zeros((D,), jnp.float32), 'upd_W2': jax.random.normal(ks[7], (D, D), jnp.float32) * s(D), 'upd_b2': jnp.zeros((D,), jnp.float32)}
    _L1_gnn_all = _L1_gnn_setup()
    _L1_gnn_in = {k: v for k, v in _L1_gnn_all.items() if k in ('msg_W1', 'msg_b1', 'msg_W2', 'msg_b2', 'upd_W1', 'upd_b1', 'upd_W2', 'upd_b2')}
    del _L1_gnn_all
    return {'x': x, 'src': src, 'dst': dst, 'edge_attr_64': edge_attr_64, 'L0_gnn_W': _L0_gnn_in['W'], 'L0_gnn_b': _L0_gnn_in['b'], 'L1_gnn_msg_W1': _L1_gnn_in['msg_W1'], 'L1_gnn_msg_b1': _L1_gnn_in['msg_b1'], 'L1_gnn_msg_W2': _L1_gnn_in['msg_W2'], 'L1_gnn_msg_b2': _L1_gnn_in['msg_b2'], 'L1_gnn_upd_W1': _L1_gnn_in['upd_W1'], 'L1_gnn_upd_b1': _L1_gnn_in['upd_b1'], 'L1_gnn_upd_W2': _L1_gnn_in['upd_W2'], 'L1_gnn_upd_b2': _L1_gnn_in['upd_b2']}

def reference(x, src, dst, edge_attr_64, L0_gnn_W, L0_gnn_b, L1_gnn_msg_W1, L1_gnn_msg_b1, L1_gnn_msg_W2, L1_gnn_msg_b2, L1_gnn_upd_W1, L1_gnn_upd_b1, L1_gnn_upd_W2, L1_gnn_upd_b2):
    import jax
    import jax.numpy as jnp

    def _L0_gnn_ref(x, edge_index, W, b):
        import jax, jax.numpy as jnp
        import numpy as np
        N_NODES = 12500
        N_EDGES = 150000
        D = 64
        n = x.shape[0]
        row, col = (edge_index[0], edge_index[1])
        ones = jnp.ones((edge_index.shape[1],), dtype=x.dtype)
        deg = jax.ops.segment_sum(ones, col, num_segments=n) + 1.0
        dis = jax.lax.rsqrt(deg)
        h = x @ W
        norm = dis[row] * dis[col]
        msg = h[row] * norm[:, None]
        agg = jax.ops.segment_sum(msg, col, num_segments=n)
        agg = agg + h * (dis * dis)[:, None]
        out = agg + b
        return x + jax.nn.gelu(out, approximate=False)

    def _L1_gnn_ref(node_x, edge_x, sources, targets, msg_W1, msg_b1, msg_W2, msg_b2, upd_W1, upd_b1, upd_W2, upd_b2):
        import jax, jax.numpy as jnp
        import numpy as np
        N_NODES = 12500
        N_EDGES = 200000
        D = 64

        def _mlp(x, W1, b1, W2, b2):
            return jnp.dot(jax.nn.relu(jnp.dot(x, W1) + b1), W2) + b2
        num_nodes = node_x.shape[0]
        source_x = jnp.take(node_x, sources, axis=0)
        target_x = jnp.take(node_x, targets, axis=0)
        message_in = jnp.concatenate((source_x, target_x, edge_x), axis=1)
        message_x = _mlp(message_in, msg_W1, msg_b1, msg_W2, msg_b2)
        agg = jax.ops.segment_sum(message_x, targets, num_segments=num_nodes)
        update_in = jnp.concatenate((agg, node_x), axis=1)
        return _mlp(update_in, upd_W1, upd_b1, upd_W2, upd_b2)
    edge_index = jnp.stack([src, dst])
    h = jnp.maximum(_layernorm(x, axis=-1), 0.0)
    x = x + _L0_gnn_ref(h, edge_index, L0_gnn_W, L0_gnn_b)
    h = jnp.maximum(_layernorm(x, axis=-1), 0.0)
    x = x + _L1_gnn_ref(h, edge_attr_64, src, dst, L1_gnn_msg_W1, L1_gnn_msg_b1, L1_gnn_msg_W2, L1_gnn_msg_b2, L1_gnn_upd_W1, L1_gnn_upd_b1, L1_gnn_upd_W2, L1_gnn_upd_b2)
    return x

_drawn_inputs = setup_inputs


def setup_inputs(seed=0):
    import zlib

    import numpy as np

    out = dict(_drawn_inputs(seed))
    spreads = {'L0_gnn_b': (0.0, 0.522),
     'L1_gnn_msg_b1': (0.0, 0.1),
     'L1_gnn_msg_b2': (0.0, 0.1),
     'L1_gnn_upd_b1': (0.0, 0.8),
     'L1_gnn_upd_b2': (0.0, 0.606)}
    factors = {}
    for name, (base, spread) in spreads.items():
        noise = np.random.default_rng([zlib.crc32(name.encode()), seed]).standard_normal(out[name].shape)
        drawn = base * np.exp(spread * noise) if base else spread * noise
        out[name] = jnp.asarray(drawn.astype(out[name].dtype))
    for name, factor in factors.items():
        out[name] = (out[name] * factor).astype(out[name].dtype)
    return out
```

```python
import concourse.bass as bass
from concourse import mybir
from concourse.alu_op_type import AluOpType as ALU
from contextlib import ExitStack



def gnn_two_layers(nc: bass.Bass, x, src, dst, edge_x, l0_w, l0_b, msg_w1, msg_b1, msg_w2, msg_b2,
                   upd_w1, upd_b1, upd_w2, upd_b2, out):
    f32, i32, bf16 = mybir.dt.float32, mybir.dt.int32, mybir.dt.bfloat16
    ACT = mybir.ActivationFunctionType
    AX = mybir.AxisListType.X

    N, D = x.shape
    E = src.shape[0]
    P = 128
    NB = 50
    NP = NB * P
    NFULL, NREST = N // P, N % P
    T = 8
    SB = T * P
    NSB = -(-E // SB)
    U = 4
    NIT = NSB // U
    assert NSB % U == 0 and NP >= N + 64
    CH = -(-E // (P * P))
    COLS = CH * P
    W = 64
    PASSES = -(-N // W)
    HI = 50
    LN_EPS = 1e-5

    src_dram = nc.dram_tensor("src_by_tile", (P, COLS), i32, kind="Internal").ap()
    g_dram = nc.dram_tensor("g_rows", (NP, D), f32, kind="Internal").ap()
    a_dram = nc.dram_tensor("a_rows", (NP, D), f32, kind="Internal").ap()
    b_dram = nc.dram_tensor("b_rows", (NP, D), f32, kind="Internal").ap()
    cnt_dram = nc.dram_tensor("count_by_node", (NB, P), f32, kind="Internal").ap()

    def wide(ap, axis, n):
        shape = list(ap.shape)
        shape[axis] = n
        return ap.broadcast_to(shape)

    ctx = ExitStack()
    with ctx:
        def sb(name, shape, dt=f32):
            return ctx.enter_context(nc.sbuf_tensor(name, shape, dt))

        def sem(name):
            return ctx.enter_context(nc.semaphore(name))

        ident = sb("ident", [P, P])
        first_row = sb("first_row", [P, P])
        ones = sb("ones", [P, P])
        iota_w = sb("iota_w", [P, W])
        iota_hist = sb("iota_hist", [P, P], bf16)
        eps_t = sb("eps_t", [P, 1])
        w_l0 = sb("w_l0", [D, D])
        b_l0 = sb("b_l0", [P, D])
        w_ab = sb("w_ab", [P, 2 * D])
        b_msg1 = sb("b_msg1", [P, D])
        w_msg2 = sb("w_msg2", [D + 1, D])
        w_upd1 = sb("w_upd1", [P, D])
        b_upd1 = sb("b_upd1", [D, 1])
        w_upd2 = sb("w_upd2", [D + 1, D])
        raw = sb("raw", [P, CH, P], i32)
        rawf = sb("rawf", [P, CH, P])
        srci = sb("srci", [P, COLS], i32)
        dstf = sb("dstf", [P, COLS])
        rel = sb("rel", [P, NSB, T])
        tmp_e = sb("tmp_e", [P, NSB, T])
        base_fast = sb("base_fast", [P, NSB])
        base = sb("base", [P, NSB])
        base_i = sb("base_i", [1, NSB], i32)
        base_pass = sb("base_pass", [P, NSB])
        bad = sb("bad", [P, 1])
        general = sb("general", [P, 1])
        fast = sb("fast", [P, 1])
        passes_i = sb("passes_i", [1, 1], i32)
        X = sb("X", [P, NB, D])
        H = sb("H", [P, NB + 1, D])
        Y = sb("Y", [P, NB, D])
        Z = sb("Z", [P, NB, D])
        hT = sb("hT", [P, NB * P])
        dlo, dhi = hT[:, 0:COLS], hT[:, COLS:2 * COLS]
        dsti = hT[:, 2 * COLS:3 * COLS].bitcast(i32)
        acc = sb("acc", [D + 1, NP])
        s1 = sb("s1", [P, NB])
        mean = sb("mean", [P, NB])
        s2 = sb("s2", [P, NB])
        std = sb("std", [P, NB])
        rstd = sb("rstd", [P, NB])
        cnt = sb("cnt", [P, NB])
        cntT = sb("cntT", [NB, P])
        dis = sb("dis", [P, NB])
        idx = sb("idx", [P, U, T], i32)
        rows = sb("rows", [P, U, T, D])
        eo = sb("eo", [P, U, T, 2 * D])
        wb = sb("wb", [P, U, D])
        eoT = sb("eoT", [P, 2, T, P])
        msg = sb("msg", [P, 2, T, D])
        one_lo = sb("one_lo", [P, 2, T, P], bf16)
        one_hi = sb("one_hi", [P, 2, T, HI], bf16)
        zeros = sb("zeros", [P, P], bf16)
        psum = ctx.enter_context(nc.psum_tensor("psum", [P, 8, 512], f32))

        wT = hT

        s_const = sem("s_const")
        s_pad = sem("s_pad")
        s_raw = [sem("s_raw_dst"), sem("s_raw_src")]
        s_x = sem("s_x")
        s_wt = sem("s_wt")
        s_tab = sem("s_tab")
        s_v = sem("s_v")
        s_rawf = sem("s_rawf")
        s_tabT = sem("s_tabT")
        s_srci = sem("s_srci")
        s_srcd = sem("s_srcd")
        s_dst_ready = sem("s_dst_ready")
        s_lohi = sem("s_lohi")
        s_basep = sem("s_basep")
        s_bad = sem("s_bad")
        s_badp = sem("s_badp")
        s_mode = sem("s_mode")
        s_oh = sem("s_oh")
        s_hfree = sem("s_hfree")
        s_hist = sem("s_hist")
        s_var = [sem("s_var0"), sem("s_var1")]
        s_std = [sem("s_std0"), sem("s_std1")]
        s_hready = [sem("s_hready0"), sem("s_hready1")]
        s_tr = sem("s_tr")
        s_trc = sem("s_trc")
        s_mm = sem("s_mm")
        s_mmc = sem("s_mmc")
        s_cntT = sem("s_cntT")
        s_cntTc = sem("s_cntTc")
        s_cntd = sem("s_cntd")
        s_cntr = sem("s_cntr")
        s_gd = sem("s_gd")
        s_abd = sem("s_abd")
        s_stT = sem("s_stT")
        s_stc = sem("s_stc")
        s_gelu_in = sem("s_gelu_in")
        s_gelu = sem("s_gelu")
        s_deg = sem("s_deg")
        s_dsq = sem("s_dsq")
        s_dis = sem("s_dis")
        s_acc0 = sem("s_acc0")
        s_wc = sem("s_wc")
        s_pass = [sem("s_pass0"), sem("s_pass1")]
        s_pdone = [sem("s_pdone0"), sem("s_pdone1")]
        s_u1 = sem("s_u1")
        s_u1c = sem("s_u1c")
        s_u2 = sem("s_u2")
        s_u2c = sem("s_u2c")
        s_u3 = sem("s_u3")
        s_u3c = sem("s_u3c")
        s_aclr = sem("s_aclr")
        s_one_row = sem("s_one_row")
        s_turn = [sem("s_turn_pool"), sem("s_turn_sp"), sem("s_turn_dve")]
        s_out = sem("s_out")
        idx_in = [[sem(f"idx_in{l}_{k}") for k in range(U)] for l in range(2)]
        gathered = [[sem(f"gathered{l}_{k}") for k in range(U)] for l in range(2)]
        rows_free = [sem(f"rows_free{l}") for l in range(2)]
        onehot = [sem(f"onehot{l}") for l in range(2)]
        summed = [sem(f"summed{l}") for l in range(2)]
        acc_add = [sem(f"acc_add{l}") for l in range(2)]
        e_in = [sem(f"e_in{k}") for k in range(U)]
        b_in = [sem(f"b_in{k}") for k in range(U)]
        transposed = sem("transposed")
        eoT_ready = sem("eoT_ready")
        pre_done = sem("pre_done")
        added = sem("added")
        relu_done = sem("relu_done")

        E_ROWS = E // P - (CH - 1) * P
        E_REST = E - (E // P) * P
        src_v, dst_v = (t[0:(CH - 1) * P * P].rearrange("(c q e) -> q c e", q=P, e=P) for t in (src, dst))
        TAIL = E // P * P

        def edge_row0(s):
            return s * SB

        block = ctx.enter_context(nc.Block())

        @block.sync
        def _(sp):
            sp.wait_ge(s_pad, 1)
            for n, (view, t) in enumerate(((dst_v, dst), (src_v, src))):
                if n:
                    sp.wait_ge(s_rawf, 1)
                sp.dma_start(raw[:, 0:CH - 1, :], view).then_inc(s_raw[n], 16)
                sp.dma_start(raw[0:E_ROWS, CH - 1, :],
                             t[(CH - 1) * P * P:TAIL].rearrange("(q e) -> q e", e=P)).then_inc(s_raw[n], 16)
                sp.dma_start(raw[E_ROWS:E_ROWS + 1, CH - 1, 0:E_REST],
                             t[TAIL:E].rearrange("(q e) -> q e", q=1)).then_inc(s_raw[n], 16)
                if n == 0:
                    sp.wait_ge(s_pad, 2)
                    sp.dma_start(X[:, 0:NFULL, :], x[0:NFULL * P, :].rearrange("(b p) d -> p b d", p=P)).then_inc(s_x, 16)
                    sp.dma_start(X[0:NREST, NFULL, :], x[NFULL * P:N, :]).then_inc(s_x, 16)
                    for w_to, w_from in (
                            (w_l0[:, :], l0_w), (w_msg2[0:D, :], msg_w2), (w_msg2[D:D + 1, :], msg_b2.rearrange("(a d) -> a d", a=1)),
                            (w_upd1[:, :], upd_w1), (w_upd2[0:D, :], upd_w2), (w_upd2[D:D + 1, :], upd_b2.rearrange("(a d) -> a d", a=1)),
                            (b_upd1[:, :], upd_b1.rearrange("(d a) -> d a", a=1)),
                            (w_ab[D:2 * D, 0:D], msg_w1[0:D, :]), (w_ab[D:2 * D, D:2 * D], msg_w1[D:2 * D, :]),
                            (b_l0[:, :], wide(l0_b.rearrange("(a d) -> a d", a=1), 0, P)),
                            (b_msg1[:, :], wide(msg_b1.rearrange("(a d) -> a d", a=1), 0, P))):
                        sp.dma_start(w_to, w_from).then_inc(s_wt, 16)
                    for k in range(U):
                        sp.dma_start(wb[0:D, k, :], msg_w1[2 * D:3 * D, :]).then_inc(s_wc, 16)
            sp.wait_ge(s_srci, 1)
            sp.dma_start(src_dram, srci[:, :]).then_inc(s_srcd, 16)
            sp.wait_ge(s_srcd, 16)
            sp.wait_ge(s_cntTc, 1)
            sp.dma_start(cnt_dram, cntT[:, :]).then_inc(s_cntd, 16)
            sp.wait_ge(s_cntd, 16)
            sp.wait_ge(s_acc0, 1)
            sp.dma_start(acc[D:D + 1, :], cnt_dram.rearrange("(a b) p -> a (b p)", a=1)).then_inc(s_cntr, 16)
            sp.wait_ge(s_mmc, NB // T + 1)
            sp.dma_start(g_dram.rearrange("(b p) d -> p b d", p=P), Y[:, :, :]).then_inc(s_gd, 16)

            sp.wait_ge(s_mode, 1)
            passes = sp.value_load(passes_i[0:1, 0:1], min_val=1, max_val=PASSES)
            with sp.Fori(0, passes) as r:
                with sp.Fori(0, NIT) as i:
                    for k in range(U):
                        sp.wait_ge(rows_free[0], r * NSB + i * U + k + 1)
                        sp.dma_start(idx[:, k, :], src_dram[:, bass.ds((i * U + k) * T, T)]).then_inc(idx_in[0][k], 16)

            sp.wait_ge(s_mmc, 2 * (NB // T + 1))
            sp.dma_start(a_dram.rearrange("(b p) d -> p b d", p=P), Y[:, :, :]).then_inc(s_abd, 16)
            sp.dma_start(b_dram.rearrange("(b p) d -> p b d", p=P), Z[:, :, :]).then_inc(s_abd, 16)
            sp.wait_ge(s_abd, 32)

            def load_superblock(r, s, k, tiles, rest):
                sp.wait_ge(summed[1], r * NSB + s + 1)
                if rest is None:
                    for half in range(2):
                        sp.dma_start(eo[:, k, half * 4:half * 4 + 4, 0:D],
                                     edge_x[bass.ds(s * SB + half * 4 * P, 4 * P), :].rearrange("(t p) d -> p t d", p=P)
                                     ).then_inc(e_in[k], 16)
                else:
                    sp.dma_start(eo[:, k, 0:tiles, 0:D],
                                 edge_x[s * SB:s * SB + tiles * P, :].rearrange("(t p) d -> p t d", p=P)).then_inc(e_in[k], 16)
                    sp.dma_start(eo[0:rest, k, tiles, 0:D], edge_x[s * SB + tiles * P:E, :]).then_inc(e_in[k], 16)
                b0 = sp.value_load(base_i[0:1, bass.ds(s, 1)], min_val=0, max_val=NP - W)
                sp.dma_start(wb[D:2 * D, k, :], b_dram[bass.ds(b0, W), :]).then_inc(b_in[k], 16)
                sp.wait_ge(rows_free[1], r * NSB + s + 1)
                sp.dma_start(idx[:, k, :], src_dram[:, bass.ds(s * T, T)]).then_inc(idx_in[1][k], 16)

            with sp.Fori(0, passes) as r:
                sp.wait_ge(s_pass[1], r + 1)
                sp.sem_inc(s_turn[1], 1)
                with sp.Fori(0, NIT - 1) as i:
                    for k in range(U):
                        load_superblock(r, i * U + k, k, T, None)
                for k in range(U):
                    s = (NIT - 1) * U + k
                    left = E - s * SB
                    if left >= SB:
                        load_superblock(r, s, k, T, None)
                    else:
                        load_superblock(r, s, k, left // P, left % P)

            sp.wait_ge(s_u3c, NB // T + 1)
            sp.dma_start(out[0:NFULL * P, :].rearrange("(b p) d -> p b d", p=P), Y[:, 0:NFULL, :]).then_inc(s_out, 16)
            sp.dma_start(out[NFULL * P:N, :], Y[0:NREST, NFULL, :]).then_inc(s_out, 16)
            sp.wait_ge(s_out, 32)
            sp.wait_ge(s_cntr, 16)
            sp.wait_ge(s_gd, 16)

        @block.gpsimd
        def _(pool):
            nc.gpsimd.memset(ones[:, :], 1.0).then_inc(s_const, 1)
            nc.gpsimd.iota(iota_w[:, :], [[1, W]], base=0, channel_multiplier=0,
                           allow_small_or_imprecise_dtypes=True).then_inc(s_const, 1)
            nc.gpsimd.iota(iota_hist[:, :], [[1, P]], base=0, channel_multiplier=0,
                           allow_small_or_imprecise_dtypes=True).then_inc(s_const, 1)
            nc.gpsimd.memset(zeros[:, :], 0.0).then_inc(s_const, 1)
            pool.wait_ge(s_const, 1)
            nc.gpsimd.affine_select(out=ident[:, :], in_=ones[:, :], compare_op=ALU.is_equal, fill=0.0, base=0,
                                    pattern=[[-1, P]], channel_multiplier=1).then_inc(s_const, 1)
            nc.gpsimd.affine_select(out=first_row[:, :], in_=ones[:, :], compare_op=ALU.is_equal, fill=0.0, base=0,
                                    pattern=[[0, P]], channel_multiplier=1).then_inc(s_const, 1)
            nc.gpsimd.memset(base_pass[:, :], 0.0).then_inc(s_const, 1)
            nc.gpsimd.memset(eps_t[:, :], LN_EPS).then_inc(s_const, 1)

            pool.wait_ge(s_mode, 1)
            passes = pool.value_load(passes_i[0:1, 0:1], min_val=1, max_val=PASSES)
            for layer, table in ((0, g_dram), (1, a_dram)):
                if layer == 0:
                    pool.wait_ge(s_gd, 16)
                else:
                    pool.wait_ge(s_abd, 32)
                with pool.Fori(0, passes) as r:
                    with pool.Fori(0, NIT) as i:
                        for k in range(U):
                            pool.wait_ge(idx_in[layer][k], 16 * (r * NIT + i + 1))
                            pool.sem_inc(s_turn[0], 1)
                            for t in range(T):
                                pool.indirect_dma_start(out=rows[:, k, t, :], out_offset=None, in_=table,
                                                        in_offset=bass.IndirectOffsetOnAxis(ap=idx[:, k, t:t + 1], axis=0)
                                                        ).then_inc(gathered[layer][k], 16)

        @block.vector
        def _(dve):
            chain = [0]

            def link(ins):
                chain[0] += 1
                ins.then_inc(s_v, 1)
                dve.wait_ge(s_v, chain[0])

            V = nc.vector
            V.memset(raw[:, CH - 1, :], -1000).then_inc(s_pad, 1)
            V.memset(X[:, :, :], 0.0).then_inc(s_pad, 1)
            link(V.memset(H[:, :, :], 0.0))
            link(V.memset(acc[:, :], 0.0))
            V.memset(eo[:, :, :, :], 0.0).then_inc(s_acc0, 1)
            dve.wait_ge(s_const, 8)
            dve.wait_ge(s_raw[0], 48)
            link(V.tensor_copy(rawf[:, :, :], raw[:, :, :]))
            V.memset(raw[:, CH - 1, :], 0).then_inc(s_rawf, 1)
            for c in range(0, CH, 4):
                m = min(4, CH - c)
                dve.wait_ge(s_tabT, c // 4 + 1)
                link(V.tensor_copy(dsti[:, c * P:(c + m) * P], psum[:, c // 4, 0:m * P]))
                link(V.tensor_copy(dstf[:, c * P:(c + m) * P], psum[:, c // 4, 0:m * P]))
            V.memset(s1[:, :], 0.0).then_inc(s_dst_ready, 1)
            link(V.tensor_scalar(dsti[:, :], dsti[:, :], 127, None, ALU.bitwise_and))
            link(V.tensor_copy(dlo[:, :], dsti[:, :]))
            link(V.tensor_tensor(dhi[:, :], dstf[:, :], dlo[:, :], ALU.subtract))
            link(V.tensor_scalar(dhi[:, :], dhi[:, :], 1.0 / P, None, ALU.mult))
            with dve.Fori(0, NSB // 2) as i:
                for k in range(2):
                    dve.wait_ge(s_hfree, 2 * i + k + 1)
                    for t in range(T):
                        col = (2 * i + k) * T + t
                        V.tensor_scalar(one_lo[:, k, t, :], iota_hist[:, :], dlo[:, bass.ds(col, 1)], None, ALU.is_equal)
                        last = V.tensor_scalar(one_hi[:, k, t, :], iota_hist[:, 0:HI], dhi[:, bass.ds(col, 1)], None, ALU.is_equal)
                    last.then_inc(s_oh, 1)
            dve.wait_ge(s_raw[1], 48)
            V.tensor_copy(rawf[:, :, :], raw[:, :, :]).then_inc(s_rawf, 1)
            for c in range(0, CH, 4):
                m = min(4, CH - c)
                dve.wait_ge(s_tabT, (CH + 3) // 4 + c // 4 + 1)
                ins = V.tensor_copy(srci[:, c * P:(c + m) * P], psum[:, c // 4, 0:m * P])
            ins.then_inc(s_srci, 1)
            dve.wait_ge(s_basep, 1)
            link(V.tensor_copy(base_fast[:, :], psum[:, 5, 0:NSB]))
            dst3 = dstf[:, 0:NSB * T].rearrange("p (s t) -> p s t", t=T)
            fast3 = wide(base_fast[:, :].rearrange("p (s t) -> p s t", t=1), 2, T)
            link(V.tensor_tensor(rel[:, :, :], dst3, fast3, ALU.subtract))
            link(V.tensor_scalar(tmp_e[:, :, :], rel[:, :, :], float(W), None, ALU.is_ge))
            link(V.tensor_reduce(bad[:, :], tmp_e[:, :, :], mybir.AxisListType.XY, ALU.add))
            link(V.tensor_scalar(tmp_e[:, :, :], rel[:, :, :], 0.0, None, ALU.is_lt))
            link(V.scalar_tensor_tensor(tmp_e[:, :, :], dst3, 0.0, tmp_e[:, :, :], ALU.is_ge, ALU.mult))
            link(V.tensor_reduce(general[:, :], tmp_e[:, :, :], mybir.AxisListType.XY, ALU.add))
            V.tensor_tensor(bad[:, :], bad[:, :], general[:, :], ALU.add).then_inc(s_bad, 1)
            dve.wait_ge(s_badp, 1)
            link(V.tensor_scalar(general[:, :], psum[:, 6, 0:1], 0.5, None, ALU.is_ge))
            link(V.tensor_scalar(fast[:, :], general[:, :], -1.0, 1.0, ALU.mult, ALU.add))
            V.tensor_scalar(passes_i[:, :], general[0:1, :], float(PASSES - 1), 1.0, ALU.mult, ALU.add).then_inc(s_mode, 1)
            dve.wait_ge(s_hist, 1)
            link(V.tensor_copy(cnt[:, :], psum[:, 4, 0:NB]))
            V.tensor_scalar(s2[:, :], cnt[:, :], 1.0, None, ALU.add).then_inc(s_deg, 1)
            dve.wait_ge(s_dsq, 1)
            V.reciprocal(dis[:, :], std[:, :]).then_inc(s_dis, 1)
            dve.wait_ge(s_dis, 1)
            dve.wait_ge(s_cntT, 1)
            V.tensor_copy(cntT[:, :], psum[0:NB, 5, 0:P]).then_inc(s_cntTc, 1)

            def bc(t):
                return wide(t[:, :].rearrange("p (b d) -> p b d", d=1), 2, D)

            def layer_norm_relu(n):
                link(V.tensor_reduce(s1[:, :], X[:, :, :], AX, ALU.add))
                link(V.tensor_scalar(mean[:, :], s1[:, :], 1.0 / D, None, ALU.mult))
                link(V.tensor_tensor(Y[:, :, :], X[:, :, :], bc(mean), ALU.subtract))
                link(V.tensor_tensor(Z[:, :, :], Y[:, :, :], Y[:, :, :], ALU.mult))
                V.tensor_reduce(s2[:, :], Z[:, :, :], AX, ALU.add).then_inc(s_var[n], 1)
                dve.wait_ge(s_std[n], 1)
                link(V.reciprocal(rstd[:, :], std[:, :]))
                V.scalar_tensor_tensor(H[:, 1:NB + 1, :], Y[:, :, :], 0.0, bc(rstd), ALU.max, ALU.mult).then_inc(s_hready[n], 1)

            def edge_pass_setup(r, layer):
                link_r(V.tensor_scalar(tmp_e[:, :, 0], base_pass[:, :], general[:, :], None, ALU.mult))
                link_r(V.scalar_tensor_tensor(base[:, :], base_fast[:, :], fast[:, :], tmp_e[:, :, 0], ALU.mult, ALU.add))
                link_r(V.tensor_copy(base_i[:, :], base[0:1, :]))
                link_r(V.tensor_scalar(base_pass[:, :], base_pass[:, :], float(W), None, ALU.add))
                base3 = wide(base[:, :].rearrange("p (s t) -> p s t", t=1), 2, T)
                V.tensor_tensor(rel[:, :, :], dst3, base3, ALU.subtract).then_inc(s_pass[layer], 1)
                dve.wait_ge(s_pass[layer], r + 1)
                dve.sem_inc(s_turn[2], 1)

            s_setup = [None]

            def link_r(ins):
                n, r, s, per = s_setup[0]
                s_setup[0] = (n + 1, r, s, per)
                ins.then_inc(s, 1)
                dve.wait_ge(s, r * per + n + 1)

            def window_onehots(s, out_slot):
                for t in range(T):
                    ins = V.tensor_scalar(out_slot[:, t, D:2 * D], iota_w[:, :], rel2[:, bass.ds(s * T + t, 1)], None, ALU.is_equal)
                return ins

            rel2 = rel[:, :, :].rearrange("p s t -> p (s t)")

            dve.wait_ge(s_x, 32)
            layer_norm_relu(0)
            for c in range(0, NB, 4):
                m = min(4, NB - c)
                dve.wait_ge(s_tr, c // 4 + 1)
                V.tensor_copy(hT[0:D, c * P:(c + m) * P], psum[0:D, (c // 4) % 2, 0:m * P]).then_inc(s_trc, 1)
            for c in range(0, NB, T):
                m = min(T, NB - c)
                dve.wait_ge(s_mm, c // T + 1)
                g3 = wide(dis[:, c:c + m].rearrange("p (b d) -> p b d", d=1), 2, D)
                V.tensor_tensor(Y[:, c:c + m, :], psum[:, 2 + (c // T) % 2, 0:m * D].rearrange("p (b d) -> p b d", d=D), g3,
                                ALU.mult).then_inc(s_mmc, 1)

            passes = dve.value_load(passes_i[0:1, 0:1], min_val=1, max_val=PASSES)
            for layer in range(2):
                if layer == 1:
                    link(V.memset(base_pass[:, :], 0.0))
                    link(V.memset(acc[0:D, :], 0.0))
                with dve.Fori(0, passes) as r:
                    s_setup[0] = (0, r, s_pdone[layer], 4)
                    edge_pass_setup(r, layer)
                    with dve.Fori(0, NIT) as i:
                        for k in range(U):
                            n = r * NSB + i * U + k
                            s = i * U + k
                            dve.wait_ge(summed[layer], n + 1)
                            window_onehots(s, eo[:, k]).then_inc(onehot[layer], 1)
                            if layer == 1:
                                dve.wait_ge(gathered[1][k], 16 * T * (r * NIT + i + 1))
                                dve.wait_ge(pre_done, n + 1)
                                V.tensor_tensor(msg[:, k % 2, :, :], psum[:, 4 + k % 2, :].rearrange("p (t d) -> p t d", d=D),
                                                rows[:, k, :, :], ALU.add).then_inc(added, 1)
                            b0 = dve.value_load(base_i[0:1, bass.ds(s, 1)], min_val=0, max_val=NP - W)
                            dve.wait_ge(summed[layer], n + U + 1)
                            V.tensor_tensor(acc[0:D, bass.ds(b0, W)], acc[0:D, bass.ds(b0, W)], psum[0:D, 6 + k % 2, 0:W],
                                            ALU.add).then_inc(acc_add[layer], 1)
                            dve.wait_ge(acc_add[layer], n + 3)
                if layer == 0:
                    V.memset(s1[:, :], 0.0).then_inc(s_stc, 1)
                    for c in range(0, NB, T):
                        m = min(T, NB - c)
                        dve.wait_ge(s_stT, c // T + 1)
                        V.tensor_tensor(Z[:, c:c + m, :], psum[:, (c // T) % 2, 0:m * D].rearrange("p (b d) -> p b d", d=D),
                                        Y[:, c:c + m, :], ALU.add).then_inc(s_stc, 1)
                    link(V.tensor_tensor(X[:, :, :], X[:, :, :], H[:, 1:NB + 1, :], ALU.add))
                    dve.wait_ge(s_stc, (NB + T - 1) // T + 1)
                    link(V.tensor_tensor(Z[:, :, :], Z[:, :, :], bc(dis), ALU.mult))
                    dve.wait_ge(s_wt, 11 * 16)
                    b3 = wide(b_l0[:, :].rearrange("p (b d) -> p b d", b=1), 1, NB)
                    V.tensor_tensor(Z[:, :, :], Z[:, :, :], b3, ALU.add).then_inc(s_gelu_in, 1)
                    dve.wait_ge(s_gelu, 1)
                    link(V.tensor_tensor(X[:, :, :], X[:, :, :], Z[:, :, :], ALU.add))
                    layer_norm_relu(1)
                    for c in range(0, NB, 4):
                        m = min(4, NB - c)
                        dve.wait_ge(s_tr, (NB + 3) // 4 + c // 4 + 1)
                        V.tensor_copy(hT[D:2 * D, c * P:(c + m) * P], psum[D:2 * D, (c // 4) % 2, 0:m * P]).then_inc(s_trc, 1)
                    for c in range(0, NB, T):
                        m = min(T, NB - c)
                        dve.wait_ge(s_mm, (NB + T - 1) // T + c // T + 1)
                        j = 2 + 2 * ((c // T) % 2)
                        ps3 = psum[:, j:j + 2, :].rearrange("p a (b d) -> p (a b) d", d=2 * D)[:, 0:m, :]
                        V.tensor_copy(Y[:, c:c + m, :], ps3[:, :, 0:D])
                        b1 = wide(b_msg1[:, :].rearrange("p (b d) -> p b d", b=1), 1, m)
                        V.tensor_tensor(Z[:, c:c + m, :], ps3[:, :, D:2 * D], b1, ALU.add).then_inc(s_mmc, 1)
            V.memset(s1[:, :], 0.0).then_inc(s_aclr, 1)
            for c in range(0, NP, 512):
                m = min(512, NP - c)
                q = c // 512
                dve.wait_ge(s_u1, q + 1)
                V.tensor_copy(hT[0:D, c:c + m], psum[0:D, q % 2, 0:m]).then_inc(s_u1c, 1)
            dve.wait_ge(s_u1, NP // 512 + 1)
            V.memset(acc[D:D + 1, :], 1.0).then_inc(s_one_row, 1)
            for c in range(0, NB, T):
                m = min(T, NB - c)
                dve.wait_ge(s_u3, c // T + 1)
                V.tensor_tensor(Y[:, c:c + m, :], psum[:, 4 + (c // T) % 2, 0:m * D].rearrange("p (b d) -> p b d", d=D),
                                X[:, c:c + m, :], ALU.add).then_inc(s_u3c, 1)

        @block.scalar
        def _(act):
            act.wait_ge(s_const, 8)

            def sqrt_var(n):
                act.wait_ge(s_var[n], 1)
                nc.scalar.activation(std[:, :], s2[:, :], ACT.Sqrt, bias=eps_t[:, :], scale=1.0 / D).then_inc(s_std[n], 1)

            act.wait_ge(s_deg, 1)
            nc.scalar.activation(std[:, :], s2[:, :], ACT.Sqrt).then_inc(s_dsq, 1)
            sqrt_var(0)
            act.wait_ge(s_gelu_in, 1)
            nc.scalar.activation(Z[:, :, :], Z[:, :, :], ACT.Gelu).then_inc(s_gelu, 1)
            sqrt_var(1)
            passes = act.value_load(passes_i[0:1, 0:1], min_val=1, max_val=PASSES)
            with act.Fori(0, passes) as r:
                with act.Fori(0, NIT) as i:
                    for k in range(U):
                        n = r * NSB + i * U + k
                        act.wait_ge(transposed, n + 1)
                        nc.scalar.activation(eoT[:, k % 2, 0:4, :], psum[:, 2 * (k % 2), :].rearrange("p (t e) -> p t e", e=P), ACT.Copy)
                        nc.scalar.activation(eoT[:, k % 2, 4:8, :], psum[:, 2 * (k % 2) + 1, :].rearrange("p (t e) -> p t e", e=P),
                                             ACT.Copy).then_inc(eoT_ready, 1)
                        act.wait_ge(added, n + 1)
                        nc.scalar.activation(msg[:, k % 2, :, :], msg[:, k % 2, :, :], ACT.Relu).then_inc(relu_done, 1)
            act.wait_ge(s_wt, 11 * 16)
            for c in range(0, NP, 512):
                m = min(512, NP - c)
                q = c // 512
                act.wait_ge(s_u2, q + 1)
                nc.scalar.activation(acc[0:D, c:c + m], psum[0:D, 2 + q % 2, 0:m], ACT.Relu, bias=b_upd1[:, :]).then_inc(s_u2c, 1)

        @block.tensor
        def _(pe):
            TT = nc.tensor
            pe.wait_ge(s_const, 8)

            def index_transposes(n):
                pe.wait_ge(s_rawf, n + 1)
                for c in range(CH):
                    ins = TT.transpose(psum[:, c // 4, (c % 4) * P:(c % 4 + 1) * P], rawf[:, c, :], ident[:, :])
                    if c % 4 == 3 or c == CH - 1:
                        ins.then_inc(s_tabT, 1)

            index_transposes(0)
            pe.wait_ge(s_dst_ready, 1)
            TT.matmul(psum[:, 5, 0:NSB], first_row[:, :], dstf[:, 0:NSB * T:T], start=True, stop=True).then_inc(s_basep, 1)
            TT.matmul(psum[:, 4, 0:HI], zeros[:, :], zeros[:, 0:HI], start=True, stop=False)
            pe.sem_inc(s_hfree, 2)
            with pe.Fori(0, NSB // 2) as i:
                for k in range(2):
                    pe.wait_ge(s_oh, 2 * i + k + 1)
                    for t in range(T):
                        ins = TT.matmul(psum[:, 4, 0:HI], one_lo[:, k, t, :], one_hi[:, k, t, :], start=False, stop=False)
                    ins.then_inc(s_hfree, 1)
            TT.matmul(psum[:, 4, 0:HI], zeros[:, :], zeros[:, 0:HI], start=False, stop=True).then_inc(s_hist, 1)
            index_transposes(1)
            pe.wait_ge(s_bad, 1)
            TT.matmul(psum[:, 6, 0:1], ones[:, :], bad[:, :], start=True, stop=True).then_inc(s_badp, 1)
            pe.wait_ge(s_dis, 1)
            TT.transpose(psum[0:NB, 5, 0:P], cnt[:, :], ident[:, :]).then_inc(s_cntT, 1)

            pe.wait_ge(s_hready[0], 1)
            pe.wait_ge(s_srci, 1)
            for b in range(NB):
                c = b // 4
                if b % 4 == 0 and c >= 2:
                    pe.wait_ge(s_trc, c - 1)
                ins = TT.transpose(psum[0:D, c % 2, (b % 4) * P:(b % 4 + 1) * P], H[:, b + 1, :], ident[:, :])
                if b % 4 == 3 or b == NB - 1:
                    ins.then_inc(s_tr, 1)
            pe.wait_ge(s_wt, 11 * 16)
            pe.wait_ge(s_trc, (NB + 3) // 4)
            for b in range(NB):
                c = b // T
                if b % T == 0 and c >= 2:
                    pe.wait_ge(s_mmc, c - 1)
                ins = TT.matmul(psum[:, 2 + c % 2, (b % T) * D:(b % T + 1) * D], hT[0:D, b * P:(b + 1) * P], w_l0[:, :],
                                start=True, stop=True)
                if b % T == T - 1 or b == NB - 1:
                    ins.then_inc(s_mm, 1)

            passes = pe.value_load(passes_i[0:1, 0:1], min_val=1, max_val=PASSES)
            pe.wait_ge(s_mmc, (NB + T - 1) // T)
            pe.wait_ge(s_acc0, 1)
            pe.sem_inc(summed[0], U)
            pe.sem_inc(rows_free[0], U)
            pe.sem_inc(acc_add[0], 2)
            with pe.Fori(0, passes) as r:
                with pe.Fori(0, NIT) as i:
                    for k in range(U):
                        n = r * NSB + i * U + k
                        pe.wait_ge(onehot[0], n + 1)
                        pe.wait_ge(gathered[0][k], 16 * T * (r * NIT + i + 1))
                        pe.wait_ge(acc_add[0], n + 1)
                        for t in range(T):
                            ins = TT.matmul(psum[0:D, 6 + k % 2, 0:W], rows[:, k, t, :], eo[:, k, t, D:2 * D],
                                            start=(t == 0), stop=(t == T - 1))
                        ins.then_inc(summed[0], 1)
                        pe.wait_ge(summed[0], n + U + 1)
                        pe.sem_inc(rows_free[0], 1)
            pe.wait_ge(s_stc, 1)
            for b in range(NB):
                c = b // T
                if b % T == 0 and c >= 2:
                    pe.wait_ge(s_stc, c)
                ins = TT.transpose(psum[:, c % 2, (b % T) * D:(b % T + 1) * D], acc[0:D, b * P:(b + 1) * P], ident[0:D, 0:D])
                if b % T == T - 1 or b == NB - 1:
                    ins.then_inc(s_stT, 1)
            pe.wait_ge(s_hready[1], 1)
            for b in range(NB):
                c = b // 4
                if b % 4 == 0 and c >= 2:
                    pe.wait_ge(s_trc, (NB + 3) // 4 + c - 1)
                ins = TT.transpose(psum[:, c % 2, (b % 4) * P:(b % 4 + 1) * P],
                                   H[:, b:b + 2, :].rearrange("p b d -> p (b d)"), ident[:, :])
                if b % 4 == 3 or b == NB - 1:
                    ins.then_inc(s_tr, 1)
            pe.wait_ge(s_trc, 2 * ((NB + 3) // 4))
            for b in range(NB):
                c = b // T
                if b % T == 0 and c >= 2:
                    pe.wait_ge(s_mmc, (NB + T - 1) // T + c - 1)
                j = 2 + 2 * (c % 2) + (b % T) // 4
                ins = TT.matmul(psum[:, j, (b % 4) * 2 * D:(b % 4 + 1) * 2 * D], hT[D:2 * D, b * P:(b + 1) * P], w_ab[D:2 * D, :],
                                start=True, stop=True)
                if b % T == T - 1 or b == NB - 1:
                    ins.then_inc(s_mm, 1)
            pe.wait_ge(s_mmc, 2 * ((NB + T - 1) // T))
            pe.wait_ge(s_wc, 16 * U)
            pe.sem_inc(summed[1], U)
            pe.sem_inc(rows_free[1], U)
            pe.sem_inc(acc_add[1], 2)
            with pe.Fori(0, passes) as r:
                with pe.Fori(0, NIT) as i:
                    for k in range(U):
                        n = r * NSB + i * U + k
                        v = r * NIT + i + 1
                        pe.wait_ge(onehot[1], n + 1)
                        pe.wait_ge(e_in[k], 32 * v)
                        for t in range(T):
                            ins = TT.transpose(psum[:, 2 * (k % 2) + t // 4, (t % 4) * P:(t % 4 + 1) * P], eo[:, k, t, :], ident[:, :])
                        ins.then_inc(transposed, 1)
                        pe.wait_ge(eoT_ready, n + 1)
                        pe.wait_ge(b_in[k], 16 * v)
                        for t in range(T):
                            ins = TT.matmul(psum[:, 4 + k % 2, t * D:(t + 1) * D], eoT[:, k % 2, t, :], wb[:, k, :],
                                            start=True, stop=True)
                        ins.then_inc(pre_done, 1)
                        pe.wait_ge(relu_done, n + 1)
                        pe.sem_inc(rows_free[1], 1)
                        pe.wait_ge(acc_add[1], n + 1)
                        for t in range(T):
                            ins = TT.matmul(psum[0:D, 6 + k % 2, 0:W], msg[:, k % 2, t, :], eo[:, k, t, D:2 * D],
                                            start=(t == 0), stop=(t == T - 1))
                        ins.then_inc(summed[1], 1)
            pe.wait_ge(s_aclr, 1)
            pe.wait_ge(s_cntr, 16)
            for c in range(0, NP, 512):
                m = min(512, NP - c)
                q = c // 512
                if q >= 2:
                    pe.wait_ge(s_u1c, q - 1)
                TT.matmul(psum[0:D, q % 2, 0:m], w_msg2[:, :], acc[:, c:c + m], start=True, stop=True).then_inc(s_u1, 1)
            for c in range(0, NP, 512):
                m = min(512, NP - c)
                q = c // 512
                pe.wait_ge(s_u1c, q + 1)
                if q >= 2:
                    pe.wait_ge(s_u2c, q - 1)
                TT.matmul(psum[0:D, 2 + q % 2, 0:m], w_upd1[:, :], hT[:, c:c + m], start=True, stop=True).then_inc(s_u2, 1)
            pe.wait_ge(s_u2c, NP // 512 + 1)
            pe.wait_ge(s_one_row, 1)
            for b in range(NB):
                c = b // T
                if b % T == 0 and c >= 2:
                    pe.wait_ge(s_u3c, c - 1)
                ins = TT.matmul(psum[:, 4 + c % 2, (b % T) * D:(b % T + 1) * D], acc[:, b * P:(b + 1) * P], w_upd2[:, :],
                                start=True, stop=True)
                if b % T == T - 1 or b == NB - 1:
                    ins.then_inc(s_u3, 1)


_INS = ['x', 'src', 'dst', 'edge_attr_64', 'L0_gnn_W', 'L0_gnn_b', 'L1_gnn_msg_W1', 'L1_gnn_msg_b1', 'L1_gnn_msg_W2',
        'L1_gnn_msg_b2', 'L1_gnn_upd_W1', 'L1_gnn_upd_b1', 'L1_gnn_upd_W2', 'L1_gnn_upd_b2']


def kernel(**inputs):
    import numpy as _np
    import concourse.bacc as _bacc
    from concourse import mybir as _mybir
    from concourse.bass_utils import run_bass_kernel_spmd as _run

    nc = _bacc.Bacc("TRN2", target_bir_lowering=False, num_devices=1)
    arrays, args = {}, []
    for name in _INS:
        a = _np.ascontiguousarray(inputs[name])
        arrays[f"in_{name}_dram"] = a
        args.append(nc.dram_tensor(f"in_{name}_dram", a.shape, _mybir.dt.from_np(a.dtype), kind="ExternalInput").ap())
    args.append(nc.dram_tensor("out_0_dram", inputs['x'].shape, _mybir.dt.float32, kind="ExternalOutput").ap())
    gnn_two_layers(nc, *args)
    r = _run(nc, [arrays], core_ids=[0])
    return r.results[0]["out_0_dram"]
```

```python
import concourse.bass as bass
from concourse import mybir
from concourse.alu_op_type import AluOpType as ALU
from contextlib import ExitStack



def gnn_two_layers(nc: bass.Bass, x, src, dst, edge_x, l0_w, l0_b, msg_w1, msg_b1, msg_w2, msg_b2,
                   upd_w1, upd_b1, upd_w2, upd_b2, out):
    f32, i32, bf16 = mybir.dt.float32, mybir.dt.int32, mybir.dt.bfloat16
    ACT = mybir.ActivationFunctionType
    AX = mybir.AxisListType.X

    N, D = x.shape
    E = src.shape[0]
    P = 128
    NB = 50
    NP = NB * P
    NFULL, NREST = N // P, N % P
    T = 8
    SB = T * P
    NSB = -(-E // SB)
    U = 4
    NIT = NSB // U
    assert NSB % U == 0 and NP >= N + 64
    CH = -(-E // (P * P))
    COLS = CH * P
    W = 64
    PASSES = -(-N // W)
    HI = 50
    LN_EPS = 1e-5

    src_dram = nc.dram_tensor("src_by_tile", (P, COLS), i32, kind="Internal").ap()
    g_dram = nc.dram_tensor("g_rows", (NP, D), f32, kind="Internal").ap()
    a_dram = nc.dram_tensor("a_rows", (NP, D), f32, kind="Internal").ap()
    b_dram = nc.dram_tensor("b_rows", (NP, D), f32, kind="Internal").ap()
    cnt_dram = nc.dram_tensor("count_by_node", (NB, P), f32, kind="Internal").ap()

    def wide(ap, axis, n):
        shape = list(ap.shape)
        shape[axis] = n
        return ap.broadcast_to(shape)

    ctx = ExitStack()
    with ctx:
        def sb(name, shape, dt=f32):
            return ctx.enter_context(nc.sbuf_tensor(name, shape, dt))

        def sem(name):
            return ctx.enter_context(nc.semaphore(name))

        ident = sb("ident", [P, P])
        first_row = sb("first_row", [P, P])
        ones = sb("ones", [P, P])
        iota_w = sb("iota_w", [P, W])
        digit = sb("digit", [P, P, T], bf16)
        eps_t = sb("eps_t", [P, 1])
        w_l0 = sb("w_l0", [D, D])
        b_l0 = sb("b_l0", [P, D])
        w_ab = sb("w_ab", [P, 2 * D])
        b_msg1 = sb("b_msg1", [P, D])
        w_msg2 = sb("w_msg2", [D + 1, D])
        w_upd1 = sb("w_upd1", [P, D])
        b_upd1 = sb("b_upd1", [D, 1])
        w_upd2 = sb("w_upd2", [D + 1, D])
        raw = sb("raw", [P, CH, P], i32)
        rawf = sb("rawf", [P, CH, P])
        srci = sb("srci", [P, COLS], i32)
        dstf = sb("dstf", [P, COLS])
        rel = sb("rel", [P, NSB, T])
        tmp_e = sb("tmp_e", [P, NSB, T])
        base_fast = sb("base_fast", [P, NSB])
        base = sb("base", [P, NSB])
        base_i = sb("base_i", [1, NSB], i32)
        base_pass = sb("base_pass", [P, NSB])
        bad = sb("bad", [P, 1])
        general = sb("general", [P, 1])
        fast = sb("fast", [P, 1])
        passes_i = sb("passes_i", [1, 1], i32)
        X = sb("X", [P, NB, D])
        H = sb("H", [P, NB + 1, D])
        Y = sb("Y", [P, NB, D])
        Z = sb("Z", [P, NB, D])
        hT = sb("hT", [P, NB * P])
        dlo, dhi = hT[:, 0:NSB * T], tmp_e[:, :, :].rearrange("p s t -> p (s t)")
        dsti = hT[:, COLS:2 * COLS].bitcast(i32)
        dlo_b, dhi_b = (hT[:, q * COLS:q * COLS + NSB * T // 2].bitcast(bf16) for q in (2, 3))
        acc = sb("acc", [D + 1, NP])
        s1 = sb("s1", [P, NB])
        mean = sb("mean", [P, NB])
        s2 = sb("s2", [P, NB])
        std = sb("std", [P, NB])
        rstd = sb("rstd", [P, NB])
        cnt = sb("cnt", [P, NB])
        cntT = sb("cntT", [NB, P])
        dis = sb("dis", [P, NB])
        idx = sb("idx", [P, U, T], i32)
        rows = sb("rows", [P, U, T, D])
        eo = sb("eo", [P, U, T, 2 * D])
        wb = sb("wb", [P, U, D])
        eoT = sb("eoT", [P, 2, T, P])
        msg = sb("msg", [P, 2, T, D])
        one_lo = sb("one_lo", [P, 2, P, T], bf16)
        one_hi = sb("one_hi", [P, 2, HI, T], bf16)
        zeros = sb("zeros", [P, P], bf16)
        psum = ctx.enter_context(nc.psum_tensor("psum", [P, 8, 512], f32))

        wT = hT

        s_const = sem("s_const")
        s_pad = sem("s_pad")
        s_raw = [sem("s_raw_dst"), sem("s_raw_src")]
        s_x = sem("s_x")
        s_wt = sem("s_wt")
        s_tab = sem("s_tab")
        s_v = sem("s_v")
        s_rawf = sem("s_rawf")
        s_tabT = sem("s_tabT")
        s_srci = sem("s_srci")
        s_srcd = sem("s_srcd")
        s_dst_ready = sem("s_dst_ready")
        s_lohi = sem("s_lohi")
        s_basep = sem("s_basep")
        s_bad = sem("s_bad")
        s_badp = sem("s_badp")
        s_mode = sem("s_mode")
        s_oh = sem("s_oh")
        s_hfree = sem("s_hfree")
        s_hist = sem("s_hist")
        s_var = [sem("s_var0"), sem("s_var1")]
        s_std = [sem("s_std0"), sem("s_std1")]
        s_hready = [sem("s_hready0"), sem("s_hready1")]
        s_tr = sem("s_tr")
        s_trc = sem("s_trc")
        s_mm = sem("s_mm")
        s_mmc = sem("s_mmc")
        s_cntT = sem("s_cntT")
        s_cntTc = sem("s_cntTc")
        s_cntd = sem("s_cntd")
        s_cntr = sem("s_cntr")
        s_gd = sem("s_gd")
        s_abd = sem("s_abd")
        s_stT = sem("s_stT")
        s_stc = sem("s_stc")
        s_gelu_in = sem("s_gelu_in")
        s_gelu = sem("s_gelu")
        s_deg = sem("s_deg")
        s_dsq = sem("s_dsq")
        s_dis = sem("s_dis")
        s_acc0 = sem("s_acc0")
        s_wc = sem("s_wc")
        s_pass = [sem("s_pass0"), sem("s_pass1")]
        s_pdone = [sem("s_pdone0"), sem("s_pdone1")]
        s_u1 = sem("s_u1")
        s_u1c = sem("s_u1c")
        s_u2 = sem("s_u2")
        s_u2c = sem("s_u2c")
        s_u3 = sem("s_u3")
        s_u3c = sem("s_u3c")
        s_aclr = sem("s_aclr")
        s_one_row = sem("s_one_row")
        s_turn = [sem("s_turn_pool"), sem("s_turn_sp"), sem("s_turn_dve"), sem("s_turn_pe")]
        s_out = sem("s_out")
        idx_in = [[sem(f"idx_in{l}_{k}") for k in range(U)] for l in range(2)]
        gathered = [[sem(f"gathered{l}_{k}") for k in range(U)] for l in range(2)]
        rows_free = [sem("rows_free0")]
        onehot = [sem(f"onehot{l}") for l in range(2)]
        summed = [sem(f"summed{l}") for l in range(2)]
        acc_add = [sem(f"acc_add{l}") for l in range(2)]
        e_in = [sem(f"e_in{k}") for k in range(U)]
        b_in = [sem(f"b_in{k}") for k in range(U)]
        counts_reset = [sem(f"counts_reset{l}") for l in range(2)]
        transposed = sem("transposed")
        eoT_ready = sem("eoT_ready")
        pre_done = sem("pre_done")
        added = sem("added")
        relu_done = sem("relu_done")

        E_ROWS = E // P - (CH - 1) * P
        E_REST = E - (E // P) * P
        src_v, dst_v = (t[0:(CH - 1) * P * P].rearrange("(c q e) -> q c e", q=P, e=P) for t in (src, dst))
        TAIL = E // P * P

        def ahead(i, k, a):
            return i + (k + a) // U, (k + a) % U

        def for_superblocks(eng, step):
            with eng.Fori(0, NIT - 1) as i:
                for k in range(U):
                    step(i, k, False)
            for k in range(U):
                step(NIT - 1, k, True)

        block = ctx.enter_context(nc.Block())

        @block.sync
        def _(sp):
            sp.wait_ge(s_pad, 1)
            for n, (view, t) in enumerate(((dst_v, dst), (src_v, src))):
                if n:
                    sp.wait_ge(s_rawf, 1)
                sp.dma_start(raw[:, 0:CH - 1, :], view).then_inc(s_raw[n], 16)
                sp.dma_start(raw[0:E_ROWS, CH - 1, :],
                             t[(CH - 1) * P * P:TAIL].rearrange("(q e) -> q e", e=P)).then_inc(s_raw[n], 16)
                sp.dma_start(raw[E_ROWS:E_ROWS + 1, CH - 1, 0:E_REST],
                             t[TAIL:E].rearrange("(q e) -> q e", q=1)).then_inc(s_raw[n], 16)
                if n == 0:
                    sp.wait_ge(s_pad, 2)
                    sp.dma_start(X[:, 0:NFULL, :], x[0:NFULL * P, :].rearrange("(b p) d -> p b d", p=P)).then_inc(s_x, 16)
                    sp.dma_start(X[0:NREST, NFULL, :], x[NFULL * P:N, :]).then_inc(s_x, 16)
                    for w_to, w_from in (
                            (w_l0[:, :], l0_w), (w_msg2[0:D, :], msg_w2), (w_msg2[D:D + 1, :], msg_b2.rearrange("(a d) -> a d", a=1)),
                            (w_upd1[:, :], upd_w1), (w_upd2[0:D, :], upd_w2), (w_upd2[D:D + 1, :], upd_b2.rearrange("(a d) -> a d", a=1)),
                            (b_upd1[:, :], upd_b1.rearrange("(d a) -> d a", a=1)),
                            (w_ab[D:2 * D, 0:D], msg_w1[0:D, :]), (w_ab[D:2 * D, D:2 * D], msg_w1[D:2 * D, :]),
                            (b_l0[:, :], wide(l0_b.rearrange("(a d) -> a d", a=1), 0, P)),
                            (b_msg1[:, :], wide(msg_b1.rearrange("(a d) -> a d", a=1), 0, P))):
                        sp.dma_start(w_to, w_from).then_inc(s_wt, 16)
                    for k in range(U):
                        sp.dma_start(wb[0:D, k, :], msg_w1[2 * D:3 * D, :]).then_inc(s_wc, 16)
            sp.wait_ge(s_srci, 1)
            sp.dma_start(src_dram, srci[:, :]).then_inc(s_srcd, 16)
            sp.wait_ge(s_srcd, 16)
            sp.wait_ge(s_cntTc, 1)
            sp.dma_start(cnt_dram, cntT[:, :]).then_inc(s_cntd, 16)
            sp.wait_ge(s_cntd, 16)
            sp.wait_ge(s_acc0, 1)
            sp.dma_start(acc[D:D + 1, :], cnt_dram.rearrange("(a b) p -> a (b p)", a=1)).then_inc(s_cntr, 16)
            sp.wait_ge(s_mmc, NB // T + 1)
            sp.dma_start(g_dram.rearrange("(b p) d -> p b d", p=P), Y[:, :, :]).then_inc(s_gd, 16)

            sp.wait_ge(s_mode, 1)
            passes = sp.value_load(passes_i[0:1, 0:1], min_val=1, max_val=PASSES)
            with sp.Fori(0, passes) as r:
                with sp.Fori(0, NIT) as i:
                    for k in range(U):
                        sp.wait_ge(rows_free[0], r * NSB + i * U + k + 1)
                        sp.dma_start(idx[:, k, :], src_dram[:, bass.ds((i * U + k) * T, T)]).then_inc(idx_in[0][k], 16)

            sp.wait_ge(s_mmc, 2 * (NB // T + 1))
            sp.dma_start(a_dram.rearrange("(b p) d -> p b d", p=P), Y[:, :, :]).then_inc(s_abd, 16)
            sp.dma_start(b_dram.rearrange("(b p) d -> p b d", p=P), Z[:, :, :]).then_inc(s_abd, 16)
            sp.wait_ge(s_abd, 32)

            def load_superblock(r, s, k, tiles, rest):
                sp.wait_ge(summed[1], r * NSB + s + 1)
                if rest is None:
                    for half in range(2):
                        sp.dma_start(eo[:, k, half * 4:half * 4 + 4, 0:D],
                                     edge_x[bass.ds(s * SB + half * 4 * P, 4 * P), :].rearrange("(t p) d -> p t d", p=P)
                                     ).then_inc(e_in[k], 16)
                else:
                    sp.dma_start(eo[:, k, 0:tiles, 0:D],
                                 edge_x[s * SB:s * SB + tiles * P, :].rearrange("(t p) d -> p t d", p=P)).then_inc(e_in[k], 16)
                    sp.dma_start(eo[0:rest, k, tiles, 0:D], edge_x[s * SB + tiles * P:E, :]).then_inc(e_in[k], 16)
                b0 = sp.value_load(base_i[0:1, bass.ds(s, 1)], min_val=0, max_val=NP - W)
                sp.dma_start(wb[D:2 * D, k, :], b_dram[bass.ds(b0, W), :]).then_inc(b_in[k], 16)
                sp.wait_ge(added, r * NSB + s + 1)
                sp.dma_start(idx[:, k, :], src_dram[:, bass.ds(s * T, T)]).then_inc(idx_in[1][k], 16)

            with sp.Fori(0, passes) as r:
                sp.wait_ge(s_pass[1], r + 1)
                sp.sem_inc(s_turn[1], 1)
                with sp.Fori(0, NIT - 1) as i:
                    for k in range(U):
                        load_superblock(r, i * U + k, k, T, None)
                for k in range(U):
                    s = (NIT - 1) * U + k
                    left = E - s * SB
                    if left >= SB:
                        load_superblock(r, s, k, T, None)
                    else:
                        load_superblock(r, s, k, left // P, left % P)

            sp.wait_ge(s_u3c, NB // T + 1)
            sp.dma_start(out[0:NFULL * P, :].rearrange("(b p) d -> p b d", p=P), Y[:, 0:NFULL, :]).then_inc(s_out, 16)
            sp.dma_start(out[NFULL * P:N, :], Y[0:NREST, NFULL, :]).then_inc(s_out, 16)
            sp.wait_ge(s_out, 32)
            sp.wait_ge(s_cntr, 16)
            sp.wait_ge(s_gd, 16)

        @block.gpsimd
        def _(pool):
            nc.gpsimd.memset(ones[:, :], 1.0).then_inc(s_const, 1)
            nc.gpsimd.iota(iota_w[:, :], [[1, W]], base=0, channel_multiplier=0,
                           allow_small_or_imprecise_dtypes=True).then_inc(s_const, 1)
            nc.gpsimd.iota(digit[:, :, :], [[1, P], [0, T]], base=0, channel_multiplier=0,
                           allow_small_or_imprecise_dtypes=True).then_inc(s_const, 1)
            nc.gpsimd.memset(zeros[:, :], 0.0).then_inc(s_const, 1)
            pool.wait_ge(s_const, 1)
            nc.gpsimd.affine_select(out=ident[:, :], in_=ones[:, :], compare_op=ALU.is_equal, fill=0.0, base=0,
                                    pattern=[[-1, P]], channel_multiplier=1).then_inc(s_const, 1)
            nc.gpsimd.affine_select(out=first_row[:, :], in_=ones[:, :], compare_op=ALU.is_equal, fill=0.0, base=0,
                                    pattern=[[0, P]], channel_multiplier=1).then_inc(s_const, 1)
            nc.gpsimd.memset(base_pass[:, :], 0.0).then_inc(s_const, 1)
            nc.gpsimd.memset(eps_t[:, :], LN_EPS).then_inc(s_const, 1)

            pool.wait_ge(s_mode, 1)
            passes = pool.value_load(passes_i[0:1, 0:1], min_val=1, max_val=PASSES)
            for layer, table in ((0, g_dram), (1, a_dram)):
                if layer == 0:
                    pool.wait_ge(s_gd, 16)
                else:
                    pool.wait_ge(s_abd, 32)
                used = (summed[0], added)[layer]
                pool.sem_inc(counts_reset[layer], 1)
                with pool.Fori(0, passes) as r:
                    with pool.Fori(0, NIT) as i:
                        for k in range(U):
                            pool.wait_ge(idx_in[layer][k], 16 * (r * NIT + i + 1))
                            pool.sem_inc(s_turn[0], 1)
                            for t in range(T):
                                pool.indirect_dma_start(out=rows[:, k, t, :], out_offset=None, in_=table,
                                                        in_offset=bass.IndirectOffsetOnAxis(ap=idx[:, k, t:t + 1], axis=0)
                                                        ).then_inc(gathered[layer][k], 16)
                    pool.wait_ge(used, (r + 1) * NSB + U)
                    pool.sem_inc(s_turn[0], 1)
                    pool.inc_swdge_sem(gathered[layer], [16 * T * NIT] * U, mode="sub")
                    pool.sem_inc(counts_reset[layer], 1)

        @block.vector
        def _(dve):
            chain = [0]

            def link(ins):
                chain[0] += 1
                ins.then_inc(s_v, 1)
                dve.wait_ge(s_v, chain[0])

            V = nc.vector
            V.memset(raw[:, CH - 1, :], -1000).then_inc(s_pad, 1)
            V.memset(X[:, :, :], 0.0).then_inc(s_pad, 1)
            link(V.memset(H[:, :, :], 0.0))
            link(V.memset(acc[:, :], 0.0))
            V.memset(eo[:, :, :, :], 0.0).then_inc(s_acc0, 1)
            dve.wait_ge(s_const, 8)
            dve.wait_ge(s_raw[0], 48)
            link(V.tensor_copy(rawf[:, :, :], raw[:, :, :]))
            V.memset(raw[:, CH - 1, :], 0).then_inc(s_rawf, 1)
            for c in range(0, CH, 4):
                m = min(4, CH - c)
                dve.wait_ge(s_tabT, c // 4 + 1)
                link(V.tensor_copy(dsti[:, c * P:(c + m) * P], psum[:, c // 4, 0:m * P]))
                link(V.tensor_copy(dstf[:, c * P:(c + m) * P], psum[:, c // 4, 0:m * P]))
            V.memset(s1[:, :], 0.0).then_inc(s_dst_ready, 1)
            link(V.tensor_scalar(dsti[:, :], dsti[:, :], 127, None, ALU.bitwise_and))
            link(V.tensor_copy(dlo, dsti[:, 0:NSB * T]))
            link(V.tensor_tensor(dhi, dstf[:, 0:NSB * T], dlo, ALU.subtract))
            link(V.tensor_scalar(dhi_b, dhi, 1.0 / P, None, ALU.mult))
            link(V.tensor_copy(dlo_b, dlo))
            with dve.Fori(0, NSB // 2) as i:
                for k in range(2):
                    dve.wait_ge(s_hfree, 2 * i + k + 1)
                    cols = bass.ds((2 * i + k) * T, T)
                    V.tensor_tensor(one_lo[:, k, :, :], digit[:, :, :],
                                    wide(dlo_b[:, cols].rearrange("p (c t) -> p c t", c=1), 1, P), ALU.is_equal)
                    last = V.tensor_tensor(one_hi[:, k, :, :], digit[:, 0:HI, :],
                                           wide(dhi_b[:, cols].rearrange("p (c t) -> p c t", c=1), 1, HI), ALU.is_equal)
                    last.then_inc(s_oh, 1)
            dve.wait_ge(s_raw[1], 48)
            V.tensor_copy(rawf[:, :, :], raw[:, :, :]).then_inc(s_rawf, 1)
            for c in range(0, CH, 4):
                m = min(4, CH - c)
                dve.wait_ge(s_tabT, (CH + 3) // 4 + c // 4 + 1)
                ins = V.tensor_copy(srci[:, c * P:(c + m) * P], psum[:, c // 4, 0:m * P])
            ins.then_inc(s_srci, 1)
            dve.wait_ge(s_basep, 1)
            link(V.tensor_copy(base_fast[:, :], psum[:, 5, 0:NSB]))
            dst3 = dstf[:, 0:NSB * T].rearrange("p (s t) -> p s t", t=T)
            fast3 = wide(base_fast[:, :].rearrange("p (s t) -> p s t", t=1), 2, T)
            link(V.tensor_tensor(rel[:, :, :], dst3, fast3, ALU.subtract))
            link(V.tensor_scalar(tmp_e[:, :, :], rel[:, :, :], float(W), None, ALU.is_ge))
            link(V.tensor_reduce(bad[:, :], tmp_e[:, :, :], mybir.AxisListType.XY, ALU.add))
            link(V.tensor_scalar(tmp_e[:, :, :], rel[:, :, :], 0.0, None, ALU.is_lt))
            link(V.scalar_tensor_tensor(tmp_e[:, :, :], dst3, 0.0, tmp_e[:, :, :], ALU.is_ge, ALU.mult))
            link(V.tensor_reduce(general[:, :], tmp_e[:, :, :], mybir.AxisListType.XY, ALU.add))
            V.tensor_tensor(bad[:, :], bad[:, :], general[:, :], ALU.add).then_inc(s_bad, 1)
            dve.wait_ge(s_badp, 1)
            link(V.tensor_scalar(general[:, :], psum[:, 6, 0:1], 0.5, None, ALU.is_ge))
            link(V.tensor_scalar(fast[:, :], general[:, :], -1.0, 1.0, ALU.mult, ALU.add))
            V.tensor_scalar(passes_i[:, :], general[0:1, :], float(PASSES - 1), 1.0, ALU.mult, ALU.add).then_inc(s_mode, 1)
            dve.wait_ge(s_hist, 1)
            link(V.tensor_copy(cnt[:, :], psum[:, 4, 0:NB]))
            V.tensor_scalar(s2[:, :], cnt[:, :], 1.0, None, ALU.add).then_inc(s_deg, 1)
            dve.wait_ge(s_dsq, 1)
            V.reciprocal(dis[:, :], std[:, :]).then_inc(s_dis, 1)
            dve.wait_ge(s_dis, 1)
            dve.wait_ge(s_cntT, 1)
            V.tensor_copy(cntT[:, :], psum[0:NB, 5, 0:P]).then_inc(s_cntTc, 1)

            def bc(t):
                return wide(t[:, :].rearrange("p (b d) -> p b d", d=1), 2, D)

            def layer_norm_relu(n):
                link(V.tensor_reduce(s1[:, :], X[:, :, :], AX, ALU.add))
                link(V.tensor_scalar(mean[:, :], s1[:, :], 1.0 / D, None, ALU.mult))
                link(V.tensor_tensor(Y[:, :, :], X[:, :, :], bc(mean), ALU.subtract))
                link(V.tensor_tensor(Z[:, :, :], Y[:, :, :], Y[:, :, :], ALU.mult))
                V.tensor_reduce(s2[:, :], Z[:, :, :], AX, ALU.add).then_inc(s_var[n], 1)
                dve.wait_ge(s_std[n], 1)
                link(V.reciprocal(rstd[:, :], std[:, :]))
                V.scalar_tensor_tensor(H[:, 1:NB + 1, :], Y[:, :, :], 0.0, bc(rstd), ALU.max, ALU.mult).then_inc(s_hready[n], 1)

            def edge_pass_setup(r, layer):
                link_r(V.tensor_scalar(tmp_e[:, :, 0], base_pass[:, :], general[:, :], None, ALU.mult))
                link_r(V.scalar_tensor_tensor(base[:, :], base_fast[:, :], fast[:, :], tmp_e[:, :, 0], ALU.mult, ALU.add))
                link_r(V.tensor_copy(base_i[:, :], base[0:1, :]))
                link_r(V.tensor_scalar(base_pass[:, :], base_pass[:, :], float(W), None, ALU.add))
                base3 = wide(base[:, :].rearrange("p (s t) -> p s t", t=1), 2, T)
                V.tensor_tensor(rel[:, :, :], dst3, base3, ALU.subtract).then_inc(s_pass[layer], 1)
                dve.wait_ge(s_pass[layer], r + 1)
                dve.sem_inc(s_turn[2], 1)

            s_setup = [None]

            def link_r(ins):
                n, r, s, per = s_setup[0]
                s_setup[0] = (n + 1, r, s, per)
                ins.then_inc(s, 1)
                dve.wait_ge(s, r * per + n + 1)

            def window_onehots(s, out_slot):
                return V.tensor_tensor(out_slot[:, :, D:2 * D], wide(iota_w[:, :].rearrange("p (t c) -> p t c", t=1), 1, T),
                                       wide(rel2[:, bass.ds(s * T, T)].rearrange("p (t c) -> p t c", c=1), 2, W), ALU.is_equal)

            rel2 = rel[:, :, :].rearrange("p s t -> p (s t)")

            dve.wait_ge(s_x, 32)
            layer_norm_relu(0)
            for c in range(0, NB, 4):
                m = min(4, NB - c)
                dve.wait_ge(s_tr, c // 4 + 1)
                V.tensor_copy(hT[0:D, c * P:(c + m) * P], psum[0:D, (c // 4) % 2, 0:m * P]).then_inc(s_trc, 1)
            for c in range(0, NB, T):
                m = min(T, NB - c)
                dve.wait_ge(s_mm, c // T + 1)
                g3 = wide(dis[:, c:c + m].rearrange("p (b d) -> p b d", d=1), 2, D)
                V.tensor_tensor(Y[:, c:c + m, :], psum[:, 2 + (c // T) % 2, 0:m * D].rearrange("p (b d) -> p b d", d=D), g3,
                                ALU.mult).then_inc(s_mmc, 1)

            passes = dve.value_load(passes_i[0:1, 0:1], min_val=1, max_val=PASSES)
            for layer in range(2):
                if layer == 1:
                    link(V.memset(base_pass[:, :], 0.0))
                    link(V.memset(acc[0:D, :], 0.0))
                with dve.Fori(0, passes) as r:
                    s_setup[0] = (0, r, s_pdone[layer], 4)
                    edge_pass_setup(r, layer)
                    def onehots_of(i, k):
                        n = r * NSB + i * U + k
                        dve.wait_ge(summed[layer], n + 1)
                        window_onehots(i * U + k, eo[:, k]).then_inc(onehot[layer], 1)

                    def add_rows(i, k):
                        dve.wait_ge(gathered[1][k], 16 * T * (i + 1))
                        dve.wait_ge(pre_done, r * NSB + i * U + k + 1)
                        V.tensor_tensor(msg[:, k % 2, :, :], psum[:, 4 + k % 2, :].rearrange("p (t d) -> p t d", d=D),
                                        rows[:, k, :, :], ALU.add).then_inc(added, 1)

                    def add_sums(i, k, b0):
                        n = r * NSB + i * U + k
                        dve.wait_ge(acc_add[layer], n + 2)
                        dve.wait_ge(summed[layer], n + U + 1)
                        V.tensor_tensor(acc[0:D, bass.ds(b0, W)], acc[0:D, bass.ds(b0, W)], psum[0:D, 6 + k % 2, 0:W],
                                        ALU.add).then_inc(acc_add[layer], 1)

                    def step(i, k, last):
                        b0 = dve.value_load(base_i[0:1, bass.ds(i * U + k, 1)], min_val=0, max_val=NP - W)
                        if not last or k + 3 < U:
                            onehots_of(*ahead(i, k, 3))
                        if layer == 1:
                            add_rows(i, k)
                        add_sums(i, k, b0)

                    if layer == 1:
                        dve.wait_ge(counts_reset[1], r + 1)
                        dve.sem_inc(s_turn[2], 1)
                    for k in range(3):
                        onehots_of(0, k)
                    for_superblocks(dve, step)
                dve.wait_ge(acc_add[layer], passes * NSB + 2)
                link(V.memset(s1[:, :], 0.0))
                if layer == 0:
                    V.memset(s1[:, :], 0.0).then_inc(s_stc, 1)
                    for c in range(0, NB, T):
                        m = min(T, NB - c)
                        dve.wait_ge(s_stT, c // T + 1)
                        V.tensor_tensor(Z[:, c:c + m, :], psum[:, (c // T) % 2, 0:m * D].rearrange("p (b d) -> p b d", d=D),
                                        Y[:, c:c + m, :], ALU.add).then_inc(s_stc, 1)
                    link(V.tensor_tensor(X[:, :, :], X[:, :, :], H[:, 1:NB + 1, :], ALU.add))
                    dve.wait_ge(s_stc, (NB + T - 1) // T + 1)
                    link(V.tensor_tensor(Z[:, :, :], Z[:, :, :], bc(dis), ALU.mult))
                    dve.wait_ge(s_wt, 11 * 16)
                    b3 = wide(b_l0[:, :].rearrange("p (b d) -> p b d", b=1), 1, NB)
                    V.tensor_tensor(Z[:, :, :], Z[:, :, :], b3, ALU.add).then_inc(s_gelu_in, 1)
                    dve.wait_ge(s_gelu, 1)
                    link(V.tensor_tensor(X[:, :, :], X[:, :, :], Z[:, :, :], ALU.add))
                    layer_norm_relu(1)
                    for c in range(0, NB, 4):
                        m = min(4, NB - c)
                        dve.wait_ge(s_tr, (NB + 3) // 4 + c // 4 + 1)
                        V.tensor_copy(hT[D:2 * D, c * P:(c + m) * P], psum[D:2 * D, (c // 4) % 2, 0:m * P]).then_inc(s_trc, 1)
                    for c in range(0, NB, T):
                        m = min(T, NB - c)
                        dve.wait_ge(s_mm, (NB + T - 1) // T + c // T + 1)
                        j = 2 + 2 * ((c // T) % 2)
                        ps3 = psum[:, j:j + 2, :].rearrange("p a (b d) -> p (a b) d", d=2 * D)[:, 0:m, :]
                        V.tensor_copy(Y[:, c:c + m, :], ps3[:, :, 0:D])
                        b1 = wide(b_msg1[:, :].rearrange("p (b d) -> p b d", b=1), 1, m)
                        V.tensor_tensor(Z[:, c:c + m, :], ps3[:, :, D:2 * D], b1, ALU.add).then_inc(s_mmc, 1)
            V.memset(s1[:, :], 0.0).then_inc(s_aclr, 1)
            for c in range(0, NP, 512):
                m = min(512, NP - c)
                q = c // 512
                dve.wait_ge(s_u1, q + 1)
                V.tensor_copy(hT[0:D, c:c + m], psum[0:D, q % 2, 0:m]).then_inc(s_u1c, 1)
            dve.wait_ge(s_u1, NP // 512 + 1)
            V.memset(acc[D:D + 1, :], 1.0).then_inc(s_one_row, 1)
            for c in range(0, NB, T):
                m = min(T, NB - c)
                dve.wait_ge(s_u3, c // T + 1)
                V.tensor_tensor(Y[:, c:c + m, :], psum[:, 4 + (c // T) % 2, 0:m * D].rearrange("p (b d) -> p b d", d=D),
                                X[:, c:c + m, :], ALU.add).then_inc(s_u3c, 1)

        @block.scalar
        def _(act):
            act.wait_ge(s_const, 8)

            def sqrt_var(n):
                act.wait_ge(s_var[n], 1)
                nc.scalar.activation(std[:, :], s2[:, :], ACT.Sqrt, bias=eps_t[:, :], scale=1.0 / D).then_inc(s_std[n], 1)

            act.wait_ge(s_deg, 1)
            nc.scalar.activation(std[:, :], s2[:, :], ACT.Sqrt).then_inc(s_dsq, 1)
            sqrt_var(0)
            act.wait_ge(s_gelu_in, 1)
            nc.scalar.activation(Z[:, :, :], Z[:, :, :], ACT.Gelu).then_inc(s_gelu, 1)
            sqrt_var(1)
            passes = act.value_load(passes_i[0:1, 0:1], min_val=1, max_val=PASSES)
            with act.Fori(0, passes) as r:
                def copy_transposed(i, k, older):
                    n = r * NSB + i * U + k
                    if older:
                        act.wait_ge(pre_done, n - 1)
                    act.wait_ge(transposed, n + 1)
                    nc.scalar.activation(eoT[:, k % 2, :, :],
                                         psum[:, 2 * (k % 2):2 * (k % 2) + 2, :].rearrange("p a (t e) -> p (a t) e", e=P),
                                         ACT.Copy).then_inc(eoT_ready, 1)

                def relu(i, k):
                    act.wait_ge(added, r * NSB + i * U + k + 1 + U)
                    nc.scalar.activation(msg[:, k % 2, :, :], msg[:, k % 2, :, :], ACT.Relu).then_inc(relu_done, 1)

                def step(i, k, last):
                    if not last or k + 2 < U:
                        copy_transposed(*ahead(i, k, 2), True)
                    relu(i, k)

                copy_transposed(0, 0, False)
                copy_transposed(0, 1, False)
                for_superblocks(act, step)
            act.wait_ge(s_wt, 11 * 16)
            for c in range(0, NP, 512):
                m = min(512, NP - c)
                q = c // 512
                act.wait_ge(s_u2, q + 1)
                nc.scalar.activation(acc[0:D, c:c + m], psum[0:D, 2 + q % 2, 0:m], ACT.Relu, bias=b_upd1[:, :]).then_inc(s_u2c, 1)

        @block.tensor
        def _(pe):
            TT = nc.tensor
            pe.wait_ge(s_const, 8)

            def index_transposes(n):
                pe.wait_ge(s_rawf, n + 1)
                for c in range(CH):
                    ins = TT.transpose(psum[:, c // 4, (c % 4) * P:(c % 4 + 1) * P], rawf[:, c, :], ident[:, :])
                    if c % 4 == 3 or c == CH - 1:
                        ins.then_inc(s_tabT, 1)

            index_transposes(0)
            pe.wait_ge(s_dst_ready, 1)
            TT.matmul(psum[:, 5, 0:NSB], first_row[:, :], dstf[:, 0:NSB * T:T], start=True, stop=True).then_inc(s_basep, 1)
            TT.matmul(psum[:, 4, 0:HI], zeros[:, :], zeros[:, 0:HI], start=True, stop=False)
            pe.sem_inc(s_hfree, 2)
            with pe.Fori(0, NSB // 2) as i:
                for k in range(2):
                    pe.wait_ge(s_oh, 2 * i + k + 1)
                    for t in range(T):
                        ins = TT.matmul(psum[:, 4, 0:HI], one_lo[:, k, :, t], one_hi[:, k, :, t], start=False, stop=False)
                    ins.then_inc(s_hfree, 1)
            TT.matmul(psum[:, 4, 0:HI], zeros[:, :], zeros[:, 0:HI], start=False, stop=True).then_inc(s_hist, 1)
            index_transposes(1)
            pe.wait_ge(s_bad, 1)
            TT.matmul(psum[:, 6, 0:1], ones[:, :], bad[:, :], start=True, stop=True).then_inc(s_badp, 1)
            pe.wait_ge(s_dis, 1)
            TT.transpose(psum[0:NB, 5, 0:P], cnt[:, :], ident[:, :]).then_inc(s_cntT, 1)

            pe.wait_ge(s_hready[0], 1)
            pe.wait_ge(s_srci, 1)
            for b in range(NB):
                c = b // 4
                if b % 4 == 0 and c >= 2:
                    pe.wait_ge(s_trc, c - 1)
                ins = TT.transpose(psum[0:D, c % 2, (b % 4) * P:(b % 4 + 1) * P], H[:, b + 1, :], ident[:, :])
                if b % 4 == 3 or b == NB - 1:
                    ins.then_inc(s_tr, 1)
            pe.wait_ge(s_wt, 11 * 16)
            pe.wait_ge(s_trc, (NB + 3) // 4)
            for b in range(NB):
                c = b // T
                if b % T == 0 and c >= 2:
                    pe.wait_ge(s_mmc, c - 1)
                ins = TT.matmul(psum[:, 2 + c % 2, (b % T) * D:(b % T + 1) * D], hT[0:D, b * P:(b + 1) * P], w_l0[:, :],
                                start=True, stop=True)
                if b % T == T - 1 or b == NB - 1:
                    ins.then_inc(s_mm, 1)

            passes = pe.value_load(passes_i[0:1, 0:1], min_val=1, max_val=PASSES)
            pe.wait_ge(s_mmc, (NB + T - 1) // T)
            pe.wait_ge(s_acc0, 1)
            pe.sem_inc(summed[0], U)
            pe.sem_inc(rows_free[0], U)
            pe.sem_inc(acc_add[0], 2)
            with pe.Fori(0, passes) as r:
                pe.wait_ge(counts_reset[0], r + 1)
                pe.sem_inc(s_turn[3], 1)
                with pe.Fori(0, NIT) as i:
                    for k in range(U):
                        n = r * NSB + i * U + k
                        pe.wait_ge(onehot[0], n + 1)
                        pe.wait_ge(gathered[0][k], 16 * T * (i + 1))
                        pe.wait_ge(acc_add[0], n + 1)
                        for t in range(T):
                            ins = TT.matmul(psum[0:D, 6 + k % 2, 0:W], rows[:, k, t, :], eo[:, k, t, D:2 * D],
                                            start=(t == 0), stop=(t == T - 1))
                        ins.then_inc(summed[0], 1)
                        pe.wait_ge(summed[0], n + U + 1)
                        pe.sem_inc(rows_free[0], 1)
            pe.wait_ge(s_stc, 1)
            for b in range(NB):
                c = b // T
                if b % T == 0 and c >= 2:
                    pe.wait_ge(s_stc, c)
                ins = TT.transpose(psum[:, c % 2, (b % T) * D:(b % T + 1) * D], acc[0:D, b * P:(b + 1) * P], ident[0:D, 0:D])
                if b % T == T - 1 or b == NB - 1:
                    ins.then_inc(s_stT, 1)
            pe.wait_ge(s_hready[1], 1)
            for b in range(NB):
                c = b // 4
                if b % 4 == 0 and c >= 2:
                    pe.wait_ge(s_trc, (NB + 3) // 4 + c - 1)
                ins = TT.transpose(psum[:, c % 2, (b % 4) * P:(b % 4 + 1) * P],
                                   H[:, b:b + 2, :].rearrange("p b d -> p (b d)"), ident[:, :])
                if b % 4 == 3 or b == NB - 1:
                    ins.then_inc(s_tr, 1)
            pe.wait_ge(s_trc, 2 * ((NB + 3) // 4))
            for b in range(NB):
                c = b // T
                if b % T == 0 and c >= 2:
                    pe.wait_ge(s_mmc, (NB + T - 1) // T + c - 1)
                j = 2 + 2 * (c % 2) + (b % T) // 4
                ins = TT.matmul(psum[:, j, (b % 4) * 2 * D:(b % 4 + 1) * 2 * D], hT[D:2 * D, b * P:(b + 1) * P], w_ab[D:2 * D, :],
                                start=True, stop=True)
                if b % T == T - 1 or b == NB - 1:
                    ins.then_inc(s_mm, 1)
            pe.wait_ge(s_mmc, 2 * ((NB + T - 1) // T))
            pe.wait_ge(s_wc, 16 * U)
            pe.sem_inc(summed[1], U)
            pe.sem_inc(added, U)
            pe.sem_inc(acc_add[1], 2)
            with pe.Fori(0, passes) as r:
                def transpose_edges(i, k):
                    pe.wait_ge(onehot[1], r * NSB + i * U + k + 1)
                    pe.wait_ge(e_in[k], 32 * (r * NIT + i + 1))
                    for t in range(T):
                        ins = TT.transpose(psum[:, 2 * (k % 2) + t // 4, (t % 4) * P:(t % 4 + 1) * P], eo[:, k, t, :], ident[:, :])
                    ins.then_inc(transposed, 1)

                def edge_and_target_terms(i, k):
                    pe.wait_ge(eoT_ready, r * NSB + i * U + k + 1)
                    pe.wait_ge(b_in[k], 16 * (r * NIT + i + 1))
                    for t in range(T):
                        ins = TT.matmul(psum[:, 4 + k % 2, t * D:(t + 1) * D], eoT[:, k % 2, t, :], wb[:, k, :],
                                        start=True, stop=True)
                    ins.then_inc(pre_done, 1)

                def sum_messages(i, k):
                    n = r * NSB + i * U + k
                    pe.wait_ge(relu_done, n + 1)
                    pe.wait_ge(acc_add[1], n + 1)
                    for t in range(T):
                        ins = TT.matmul(psum[0:D, 6 + k % 2, 0:W], msg[:, k % 2, t, :], eo[:, k, t, D:2 * D],
                                        start=(t == 0), stop=(t == T - 1))
                    ins.then_inc(summed[1], 1)

                def step(i, k, last):
                    if not last or k + 2 < U:
                        transpose_edges(*ahead(i, k, 2))
                    if not last or k + 1 < U:
                        edge_and_target_terms(*ahead(i, k, 1))
                    sum_messages(i, k)

                transpose_edges(0, 0)
                transpose_edges(0, 1)
                edge_and_target_terms(0, 0)
                for_superblocks(pe, step)
            pe.wait_ge(s_aclr, 1)
            pe.wait_ge(s_cntr, 16)
            for c in range(0, NP, 512):
                m = min(512, NP - c)
                q = c // 512
                if q >= 2:
                    pe.wait_ge(s_u1c, q - 1)
                TT.matmul(psum[0:D, q % 2, 0:m], w_msg2[:, :], acc[:, c:c + m], start=True, stop=True).then_inc(s_u1, 1)
            for c in range(0, NP, 512):
                m = min(512, NP - c)
                q = c // 512
                pe.wait_ge(s_u1c, q + 1)
                if q >= 2:
                    pe.wait_ge(s_u2c, q - 1)
                TT.matmul(psum[0:D, 2 + q % 2, 0:m], w_upd1[:, :], hT[:, c:c + m], start=True, stop=True).then_inc(s_u2, 1)
            pe.wait_ge(s_u2c, NP // 512 + 1)
            pe.wait_ge(s_one_row, 1)
            for b in range(NB):
                c = b // T
                if b % T == 0 and c >= 2:
                    pe.wait_ge(s_u3c, c - 1)
                ins = TT.matmul(psum[:, 4 + c % 2, (b % T) * D:(b % T + 1) * D], acc[:, b * P:(b + 1) * P], w_upd2[:, :],
                                start=True, stop=True)
                if b % T == T - 1 or b == NB - 1:
                    ins.then_inc(s_u3, 1)


_INS = ['x', 'src', 'dst', 'edge_attr_64', 'L0_gnn_W', 'L0_gnn_b', 'L1_gnn_msg_W1', 'L1_gnn_msg_b1', 'L1_gnn_msg_W2',
        'L1_gnn_msg_b2', 'L1_gnn_upd_W1', 'L1_gnn_upd_b1', 'L1_gnn_upd_W2', 'L1_gnn_upd_b2']


def kernel(**inputs):
    import numpy as _np
    import concourse.bacc as _bacc
    from concourse import mybir as _mybir
    from concourse.bass_utils import run_bass_kernel_spmd as _run

    nc = _bacc.Bacc("TRN2", target_bir_lowering=False, num_devices=1)
    arrays, args = {}, []
    for name in _INS:
        a = _np.ascontiguousarray(inputs[name])
        arrays[f"in_{name}_dram"] = a
        args.append(nc.dram_tensor(f"in_{name}_dram", a.shape, _mybir.dt.from_np(a.dtype), kind="ExternalInput").ap())
    args.append(nc.dram_tensor("out_0_dram", inputs['x'].shape, _mybir.dt.float32, kind="ExternalOutput").ap())
    gnn_two_layers(nc, *args)
    r = _run(nc, [arrays], core_ids=[0])
    return r.results[0]["out_0_dram"]
```

```python
import concourse.bass as bass
from concourse import mybir
from concourse.alu_op_type import AluOpType as ALU
from contextlib import ExitStack



def gnn_two_layers(nc: bass.Bass, x, src, dst, edge_x, l0_w, l0_b, msg_w1, msg_b1, msg_w2, msg_b2,
                   upd_w1, upd_b1, upd_w2, upd_b2, out):
    f32, i32, bf16, fp16 = mybir.dt.float32, mybir.dt.int32, mybir.dt.bfloat16, mybir.dt.float16
    ACT = mybir.ActivationFunctionType
    AX = mybir.AxisListType.X

    N, D = x.shape
    E = src.shape[0]
    P = 128
    NB = 50
    NP = NB * P
    NFULL, NREST = N // P, N % P
    T = 8
    SB = T * P
    NSB = -(-E // SB)
    U = 4
    NIT = NSB // U
    assert NSB % U == 0 and NP >= N + 64
    CH = -(-E // (P * P))
    COLS = CH * P
    W = 64
    PASSES = -(-N // W)
    HI = 50
    LN_EPS = 1e-5
    SLOTS = 8
    HS = -(-N // P)
    KEYS = HS * SLOTS
    BT = P // SLOTS
    NPART = 3
    BW = 2 * W
    MB, MS = 10, 8
    NMIX = 7
    NCB = NMIX * MB
    S0 = NCB * BT // T
    assert S0 + NMIX * MS == NSB and MS % U == 0 and MB % 2 == 0
    ADDS = MB + MS

    src_dram = nc.dram_tensor("src_by_tile", (P, COLS), i32, kind="Internal").ap()
    g_dram = nc.dram_tensor("g_rows", (NP, D), f32, kind="Internal").ap()
    a_dram = nc.dram_tensor("a_rows", (NP, D), f32, kind="Internal").ap()
    b_dram = nc.dram_tensor("b_rows", (NP, D), f32, kind="Internal").ap()
    cnt_dram = nc.dram_tensor("count_by_node", (NB, P), f32, kind="Internal").ap()

    def wide(ap, axis, n):
        shape = list(ap.shape)
        shape[axis] = n
        return ap.broadcast_to(shape)

    ctx = ExitStack()
    with ctx:
        def sb(name, shape, dt=f32):
            return ctx.enter_context(nc.sbuf_tensor(name, shape, dt))

        def sem(name):
            return ctx.enter_context(nc.semaphore(name))

        ident = sb("ident", [P, P])
        first_row = sb("first_row", [P, P])
        ones = sb("ones", [P, P])
        iota_bw = sb("iota_bw", [P, BW])
        iota_w = iota_bw[:, 0:W]
        digit = sb("digit", [P, P, T], bf16)
        eps_t = sb("eps_t", [P, 1])
        w_l0 = sb("w_l0", [D, D])
        b_l0 = sb("b_l0", [P, D])
        w_ab = sb("w_ab", [P, 2 * D])
        b_msg1 = sb("b_msg1", [P, D])
        w_msg2 = sb("w_msg2", [D + 1, D])
        w_upd1 = sb("w_upd1", [P, D])
        b_upd1 = sb("b_upd1", [D, 1])
        w_upd2 = sb("w_upd2", [D + 1, D])
        raw = sb("raw", [P, CH, P], i32)
        rawf = sb("rawf", [P, CH, P])
        srci = sb("srci", [P, COLS], i32)
        dstf = sb("dstf", [P, COLS])
        rel = sb("rel", [P, NSB, T])
        tmp_e = sb("tmp_e", [P, NSB, T])
        base_fast = sb("base_fast", [P, NSB])
        base = sb("base", [P, NSB])
        base_i = sb("base_i", [1, NSB], i32)
        base_pass = sb("base_pass", [P, NSB])
        bad = sb("bad", [P, 1])
        general = sb("general", [P, 1])
        fast = sb("fast", [P, 1])
        passes_i = sb("passes_i", [1, 1], i32)
        X = sb("X", [P, NB, D])
        H = sb("H", [P, NB + 1, D])
        Y = sb("Y", [P, NB, D])
        Z = sb("Z", [P, NB, D])
        hT = sb("hT", [P, NB * P])
        dlo, dhi = hT[:, 0:NSB * T], tmp_e[:, :, :].rearrange("p s t -> p (s t)")
        dsti = hT[:, COLS:2 * COLS].bitcast(i32)
        dlo_b, dhi_b = (hT[:, q * COLS:q * COLS + NSB * T // 2].bitcast(bf16) for q in (2, 3))
        acc = sb("acc", [D + 1, NP])
        s1 = sb("s1", [P, NB])
        mean = sb("mean", [P, NB])
        s2 = sb("s2", [P, NB])
        std = sb("std", [P, NB])
        rstd = sb("rstd", [P, NB])
        cnt = sb("cnt", [P, NB])
        cntT = sb("cntT", [NB, P])
        dis = sb("dis", [P, NB])
        idx = sb("idx", [P, U, T], i32)
        rows = sb("rows", [P, U, T, D])
        work = sb("work", [P, (HS + 1) * NPART * D // 2])
        gtab = work[:, :].bitcast(bf16).rearrange("p (h k d) -> p h k d", k=NPART, d=D)
        eo = work[:, 0:U * T * 2 * D].rearrange("p (u t d) -> p u t d", u=U, t=T)
        wb = sb("wb", [P, U, D])
        eoT = sb("eoT", [P, 2, T, P])
        onehot0 = eoT[:, :, :, :].rearrange("p a t e -> p (a t e)").rearrange("p (u t c) -> p u t c", u=U, t=T)
        msg = sb("msg", [P, 2, T, D])
        counts = hT[:, 0:HS * P].bitcast(bf16).rearrange("p (a h m) -> p a h m", a=2, h=HS)
        keys = Z[:, :, :].rearrange("p b d -> p (b d)")[:, 0:BT * KEYS // 2].bitcast(fp16).rearrange("p (t k) -> p t k", t=BT)
        key_digit = sb("key_digit", [P, KEYS], fp16)
        key_of = raw[:, :, :].rearrange("p c e -> p (c e)")[:, 0:NSB * T].bitcast(f32)
        raw_flat = rawf[:, :, :].rearrange("p c e -> p (c e)")
        src_lo_i = raw_flat[:, 0:NSB * T].bitcast(i32)
        src_lo = raw_flat[:, 0:NSB * T // 2].bitcast(bf16)
        expand = rows[:, :, :, :].rearrange("p u t d -> p (u t d)")[:, 0:T * P].rearrange("p (q m) -> p q m", m=P)
        slot_i = sb("slot_i", [P, 1], i32)
        slot = sb("slot", [P, 1])
        slot_node = sb("slot_node", [P, CH * T])
        slot_tmp = sb("slot_tmp", [P, NCB])
        slot_abs, slot_lo_f = (sb(n, [P, CH * T]) for n in ("slot_abs", "slot_lo_f"))
        slot_abs_i, slot_lo_i = (sb(n, [P, CH * T], i32) for n in ("slot_abs_i", "slot_lo_i"))
        slot_lo_b, slot_hi_b, slot_cnt = (sb(n, [P, CH * T], bf16) for n in ("slot_lo_b", "slot_hi_b", "slot_cnt"))
        edge_slot = work[:, 0:NSB * T // BT // 2 * P // 2].bitcast(bf16).rearrange("p (b m) -> p b m", m=P)
        tile_rel = eoT[:, :, :, :].rearrange("p a t e -> p (a t e)")[:, 0:NSB * T]
        ones_b = sb("ones_b", [P, 1], bf16)
        part = sb("part", [P, 2, D])
        slot_oh = sb("slot_oh", [P, 2, BW])
        one_lo = sb("one_lo", [P, 2, P, T], bf16)
        one_hi = sb("one_hi", [P, 2, HI, T], bf16)
        zeros = sb("zeros", [P, P], bf16)
        psum = ctx.enter_context(nc.psum_tensor("psum", [P, 8, 512], f32))

        s_const = sem("s_const")
        s_pad = sem("s_pad")
        s_raw = [sem("s_raw_dst"), sem("s_raw_src")]
        s_x = sem("s_x")
        s_wt = sem("s_wt")
        s_tab = sem("s_tab")
        s_v = sem("s_v")
        s_rawf = sem("s_rawf")
        s_tabT = sem("s_tabT")
        s_srci = sem("s_srci")
        s_srcd = sem("s_srcd")
        s_dst_ready = sem("s_dst_ready")
        s_lohi = sem("s_lohi")
        s_basep = sem("s_basep")
        s_bad = sem("s_bad")
        s_badp = sem("s_badp")
        s_mode = sem("s_mode")
        s_oh = sem("s_oh")
        s_hfree = sem("s_hfree")
        s_hist = sem("s_hist")
        s_var = [sem("s_var0"), sem("s_var1")]
        s_std = [sem("s_std0"), sem("s_std1")]
        s_hready = [sem("s_hready0"), sem("s_hready1")]
        s_tr = sem("s_tr")
        s_trc = sem("s_trc")
        s_mm = sem("s_mm")
        s_mmc = sem("s_mmc")
        s_cntT = sem("s_cntT")
        s_cntTc = sem("s_cntTc")
        s_cntd = sem("s_cntd")
        s_cntr = sem("s_cntr")
        s_gd = sem("s_gd")
        s_abd = sem("s_abd")
        s_stT = sem("s_stT")
        s_stc = sem("s_stc")
        s_gelu_in = sem("s_gelu_in")
        s_gelu = sem("s_gelu")
        s_deg = sem("s_deg")
        s_dsq = sem("s_dsq")
        s_dis = sem("s_dis")
        s_acc0 = sem("s_acc0")
        s_wc = sem("s_wc")
        s_pass = [sem(f"s_pass{l}") for l in range(3)]
        s_pdone = [sem(f"s_pdone{l}") for l in range(3)]
        s_u1 = sem("s_u1")
        s_u1c = sem("s_u1c")
        s_u2 = sem("s_u2")
        s_u2c = sem("s_u2c")
        s_u3 = sem("s_u3")
        s_u3c = sem("s_u3c")
        s_aclr = sem("s_aclr")
        s_one_row = sem("s_one_row")
        s_turn = [sem("s_turn_pool"), sem("s_turn_sp"), sem("s_turn_dve"), sem("s_turn_pe")]
        s_out = sem("s_out")
        idx_in = [[sem(f"idx_in{l}_{k}") for k in range(U)] for l in range(3)]
        gathered = [[sem(f"gathered{l}_{k}") for k in range(U)] for l in range(3)]
        onehot = [sem(f"onehot{l}") for l in range(3)]
        summed = [sem(f"summed{l}") for l in range(3)]
        acc_add = [sem(f"acc_add{l}") for l in range(3)]
        key_ready = sem("key_ready")
        counted = sem("counted")
        evacuated = sem("evacuated")
        multiplied = sem("multiplied")
        part_ready = sem("part_ready")
        placed = sem("placed")
        s_gtab = sem("s_gtab")
        s_tile0 = sem("s_tile0")
        s_edgeslot = sem("s_edgeslot")
        s_slotcnt = sem("s_slotcnt")
        s_slotoh = sem("s_slotoh")
        s_slothist = sem("s_slothist")
        s_slots = sem("s_slots")
        e_in = [sem(f"e_in{k}") for k in range(U)]
        b_in = [sem(f"b_in{k}") for k in range(U)]
        counts_reset = [sem(f"counts_reset{l}") for l in range(3)]
        transposed = sem("transposed")
        eoT_ready = sem("eoT_ready")
        pre_done = sem("pre_done")
        added = sem("added")
        relu_done = sem("relu_done")

        E_ROWS = E // P - (CH - 1) * P
        E_REST = E - (E // P) * P
        src_v, dst_v = (t[0:(CH - 1) * P * P].rearrange("(c q e) -> q c e", q=P, e=P) for t in (src, dst))
        TAIL = E // P * P

        def ahead(i, k, a):
            return i + (k + a) // U, (k + a) % U

        def for_superblocks(eng, step):
            with eng.Fori(0, NIT - 1) as i:
                for k in range(U):
                    step(i, k, False)
            for k in range(U):
                step(NIT - 1, k, True)

        def mixed_bodies(eng, step):
            for j in range(MB):
                step(0, j)
            with eng.Fori(1, NMIX) as i:
                for j in range(MB):
                    step(i, j)

        def place_gathered(k):
            return 1 + 2 * k

        def place_counted(j):
            return 2 * j if j <= MS else MS + j

        block = ctx.enter_context(nc.Block())

        @block.sync
        def _(sp):
            sp.wait_ge(s_pad, 1)
            for n, (view, t) in enumerate(((dst_v, dst), (src_v, src))):
                if n:
                    sp.wait_ge(s_rawf, 1)
                sp.dma_start(raw[:, 0:CH - 1, :], view).then_inc(s_raw[n], 16)
                sp.dma_start(raw[0:E_ROWS, CH - 1, :],
                             t[(CH - 1) * P * P:TAIL].rearrange("(q e) -> q e", e=P)).then_inc(s_raw[n], 16)
                sp.dma_start(raw[E_ROWS:E_ROWS + 1, CH - 1, 0:E_REST],
                             t[TAIL:E].rearrange("(q e) -> q e", q=1)).then_inc(s_raw[n], 16)
                if n == 0:
                    sp.wait_ge(s_pad, 2)
                    sp.dma_start(X[:, 0:NFULL, :], x[0:NFULL * P, :].rearrange("(b p) d -> p b d", p=P)).then_inc(s_x, 16)
                    sp.dma_start(X[0:NREST, NFULL, :], x[NFULL * P:N, :]).then_inc(s_x, 16)
                    for w_to, w_from in (
                            (w_l0[:, :], l0_w), (w_msg2[0:D, :], msg_w2), (w_msg2[D:D + 1, :], msg_b2.rearrange("(a d) -> a d", a=1)),
                            (w_upd1[:, :], upd_w1), (w_upd2[0:D, :], upd_w2), (w_upd2[D:D + 1, :], upd_b2.rearrange("(a d) -> a d", a=1)),
                            (b_upd1[:, :], upd_b1.rearrange("(d a) -> d a", a=1)),
                            (w_ab[D:2 * D, 0:D], msg_w1[0:D, :]), (w_ab[D:2 * D, D:2 * D], msg_w1[D:2 * D, :]),
                            (b_l0[:, :], wide(l0_b.rearrange("(a d) -> a d", a=1), 0, P)),
                            (b_msg1[:, :], wide(msg_b1.rearrange("(a d) -> a d", a=1), 0, P))):
                        sp.dma_start(w_to, w_from).then_inc(s_wt, 16)
                    for k in range(U):
                        sp.dma_start(wb[0:D, k, :], msg_w1[2 * D:3 * D, :]).then_inc(s_wc, 16)
            sp.wait_ge(s_srci, 1)
            sp.dma_start(src_dram, srci[:, :]).then_inc(s_srcd, 16)
            sp.wait_ge(s_srcd, 16)
            sp.wait_ge(s_cntTc, 1)
            sp.dma_start(cnt_dram, cntT[:, :]).then_inc(s_cntd, 16)
            sp.wait_ge(s_cntd, 16)
            sp.wait_ge(s_acc0, 1)
            sp.dma_start(acc[D:D + 1, :], cnt_dram.rearrange("(a b) p -> a (b p)", a=1)).then_inc(s_cntr, 16)
            sp.wait_ge(s_mmc, NB // T + 1)
            sp.dma_start(g_dram.rearrange("(b p) d -> p b d", p=P), Y[:, :, :]).then_inc(s_gd, 16)

            sp.wait_ge(s_mode, 1)
            passes = sp.value_load(passes_i[0:1, 0:1], min_val=1, max_val=PASSES)
            with sp.Fori(0, NMIX) as i:
                for k in range(MS):
                    sp.wait_ge(summed[0], i * MS + k + 1)
                    sp.dma_start(idx[:, k % U, :], src_dram[:, bass.ds((i * MS + k + S0) * T, T)]).then_inc(idx_in[0][k % U], 16)
            with sp.If(passes > 1):
                with sp.Fori(0, passes) as r:
                    with sp.Fori(0, NIT) as i:
                        for k in range(U):
                            sp.wait_ge(summed[2], r * NSB + i * U + k + 1)
                            sp.dma_start(idx[:, k, :], src_dram[:, bass.ds((i * U + k) * T, T)]).then_inc(idx_in[2][k], 16)

            sp.wait_ge(s_mmc, 2 * (NB // T + 1))
            sp.dma_start(a_dram.rearrange("(b p) d -> p b d", p=P), Y[:, :, :]).then_inc(s_abd, 16)
            sp.dma_start(b_dram.rearrange("(b p) d -> p b d", p=P), Z[:, :, :]).then_inc(s_abd, 16)
            sp.wait_ge(s_abd, 32)

            def load_superblock(r, s, k, tiles, rest):
                sp.wait_ge(summed[1], r * NSB + s + 1)
                if rest is None:
                    for half in range(2):
                        sp.dma_start(eo[:, k, half * 4:half * 4 + 4, 0:D],
                                     edge_x[bass.ds(s * SB + half * 4 * P, 4 * P), :].rearrange("(t p) d -> p t d", p=P)
                                     ).then_inc(e_in[k], 16)
                else:
                    sp.dma_start(eo[:, k, 0:tiles, 0:D],
                                 edge_x[s * SB:s * SB + tiles * P, :].rearrange("(t p) d -> p t d", p=P)).then_inc(e_in[k], 16)
                    sp.dma_start(eo[0:rest, k, tiles, 0:D], edge_x[s * SB + tiles * P:E, :]).then_inc(e_in[k], 16)
                b0 = sp.value_load(base_i[0:1, bass.ds(s, 1)], min_val=0, max_val=NP - W)
                sp.dma_start(wb[D:2 * D, k, :], b_dram[bass.ds(b0, W), :]).then_inc(b_in[k], 16)
                sp.wait_ge(added, r * NSB + s + 1)
                sp.dma_start(idx[:, k, :], src_dram[:, bass.ds(s * T, T)]).then_inc(idx_in[1][k], 16)

            with sp.Fori(0, passes) as r:
                sp.wait_ge(s_pass[1], r + 1)
                sp.sem_inc(s_turn[1], 1)
                with sp.Fori(0, NIT - 1) as i:
                    for k in range(U):
                        load_superblock(r, i * U + k, k, T, None)
                for k in range(U):
                    s = (NIT - 1) * U + k
                    left = E - s * SB
                    if left >= SB:
                        load_superblock(r, s, k, T, None)
                    else:
                        load_superblock(r, s, k, left // P, left % P)

            sp.wait_ge(s_u3c, NB // T + 1)
            sp.dma_start(out[0:NFULL * P, :].rearrange("(b p) d -> p b d", p=P), Y[:, 0:NFULL, :]).then_inc(s_out, 16)
            sp.dma_start(out[NFULL * P:N, :], Y[0:NREST, NFULL, :]).then_inc(s_out, 16)
            sp.wait_ge(s_out, 32)
            sp.wait_ge(s_cntr, 16)
            sp.wait_ge(s_gd, 16)

        @block.gpsimd
        def _(pool):
            nc.gpsimd.memset(ones[:, :], 1.0).then_inc(s_const, 1)
            nc.gpsimd.iota(iota_bw[:, :], [[1, BW]], base=0, channel_multiplier=0,
                           allow_small_or_imprecise_dtypes=True).then_inc(s_const, 1)
            nc.gpsimd.iota(digit[:, :, :], [[1, P], [0, T]], base=0, channel_multiplier=0,
                           allow_small_or_imprecise_dtypes=True).then_inc(s_const, 1)
            nc.gpsimd.memset(zeros[:, :], 0.0).then_inc(s_const, 1)
            nc.gpsimd.memset(ones_b[:, :], 1.0)
            pool.wait_ge(s_const, 1)
            nc.gpsimd.affine_select(out=ident[:, :], in_=ones[:, :], compare_op=ALU.is_equal, fill=0.0, base=0,
                                    pattern=[[-1, P]], channel_multiplier=1).then_inc(s_const, 1)
            nc.gpsimd.affine_select(out=first_row[:, :], in_=ones[:, :], compare_op=ALU.is_equal, fill=0.0, base=0,
                                    pattern=[[0, P]], channel_multiplier=1).then_inc(s_const, 1)
            nc.gpsimd.memset(base_pass[:, :], 0.0).then_inc(s_const, 1)
            nc.gpsimd.memset(eps_t[:, :], LN_EPS).then_inc(s_const, 1)
            nc.gpsimd.iota(key_digit[:, :], [[1, KEYS]], base=0, channel_multiplier=0,
                           allow_small_or_imprecise_dtypes=True).then_inc(s_const, 1)
            nc.gpsimd.iota(slot_i[:, :], [[0, 1]], base=0, channel_multiplier=1).then_inc(s_const, 1)
            nc.gpsimd.memset(expand, 1.0).then_inc(s_const, 1)
            pool.wait_ge(s_const, 11)
            nc.gpsimd.affine_select(out=expand.rearrange("p q (j s) -> p q j s", s=SLOTS),
                                    in_=expand.rearrange("p q (j s) -> p q j s", s=SLOTS),
                                    compare_op=ALU.is_equal, fill=0.0, base=0,
                                    pattern=[[-BT, T], [-1, BT], [0, SLOTS]], channel_multiplier=1).then_inc(s_const, 1)

            nc.gpsimd.memset(acc[:, :], 0.0).then_inc(s_acc0, 1)
            pool.wait_ge(s_mode, 1)
            passes = pool.value_load(passes_i[0:1, 0:1], min_val=1, max_val=PASSES)

            def gather(ring, k, visit, table):
                pool.wait_ge(idx_in[ring][k], 16 * visit)
                pool.sem_inc(s_turn[0], 1)
                for t in range(T):
                    pool.indirect_dma_start(out=rows[:, k, t, :], out_offset=None, in_=table,
                                            in_offset=bass.IndirectOffsetOnAxis(ap=idx[:, k, t:t + 1], axis=0)
                                            ).then_inc(gathered[ring][k], 16)

            def gather_passes(ring, used, table):
                pool.sem_inc(counts_reset[ring], 1)
                with pool.Fori(0, passes) as r:
                    with pool.Fori(0, NIT) as i:
                        for k in range(U):
                            gather(ring, k, r * NIT + i + 1, table)
                    pool.wait_ge(used, (r + 1) * NSB + U)
                    pool.sem_inc(s_turn[0], 1)
                    pool.inc_swdge_sem(gathered[ring], [16 * T * NIT] * U, mode="sub")
                    pool.sem_inc(counts_reset[ring], 1)

            pool.wait_ge(s_gd, 16)
            with pool.Fori(0, NMIX) as i:
                for k in range(MS):
                    gather(0, k % U, i * (MS // U) + k // U + 1, g_dram)
            with pool.If(passes > 1):
                gather_passes(2, summed[2], g_dram)
            pool.wait_ge(s_abd, 32)
            gather_passes(1, added, a_dram)

        @block.vector
        def _(dve):
            chain = [0]

            def link(ins):
                chain[0] += 1
                ins.then_inc(s_v, 1)
                dve.wait_ge(s_v, chain[0])

            V = nc.vector
            V.memset(raw[:, CH - 1, :], -1000).then_inc(s_pad, 1)
            V.memset(X[:, :, :], 0.0).then_inc(s_pad, 1)
            link(V.memset(H[:, :, :], 0.0))
            dve.wait_ge(s_const, 12)
            dve.wait_ge(s_raw[0], 48)
            link(V.tensor_copy(rawf[:, :, :], raw[:, :, :]))
            V.memset(raw[:, CH - 1, :], 0).then_inc(s_rawf, 1)
            for c in range(0, CH, 4):
                m = min(4, CH - c)
                dve.wait_ge(s_tabT, c // 4 + 1)
                link(V.tensor_copy(dsti[:, c * P:(c + m) * P], psum[:, c // 4, 0:m * P]))
                link(V.tensor_copy(dstf[:, c * P:(c + m) * P], psum[:, c // 4, 0:m * P]))
            V.memset(s1[:, :], 0.0).then_inc(s_dst_ready, 1)
            link(V.tensor_scalar(dsti[:, :], dsti[:, :], 127, None, ALU.bitwise_and))
            link(V.tensor_copy(dlo, dsti[:, 0:NSB * T]))
            link(V.tensor_tensor(dhi, dstf[:, 0:NSB * T], dlo, ALU.subtract))
            link(V.tensor_scalar(dhi_b, dhi, 1.0 / P, None, ALU.mult))
            link(V.tensor_copy(dlo_b, dlo))
            link(V.tensor_scalar(slot_i[:, :], slot_i[:, :], SLOTS - 1, None, ALU.bitwise_and))
            link(V.tensor_copy(slot[:, :], slot_i[:, :]))
            link(V.memset(bad[:, :], 0.0))

            def count_bad(t, ap, limit, op, valid=None):
                link(V.tensor_scalar(t, ap, limit, None, op))
                if valid is not None:
                    link(V.scalar_tensor_tensor(t, valid, 0.0, t, ALU.is_ge, ALU.mult))
                link(V.tensor_reduce(general[:, :], t, AX, ALU.add))
                link(V.tensor_tensor(bad[:, :], bad[:, :], general[:, :], ALU.add))

            rel2 = rel[:, :, :].rearrange("p s t -> p (s t)")
            tmp2 = tmp_e[:, :, :].rearrange("p s t -> p (s t)")
            dst2 = dstf[:, 0:NSB * T]
            dve.wait_ge(s_tile0, 1)
            link(V.tensor_tensor(rel2, dst2, psum[:, 0:4, :].rearrange("p a e -> p (a e)")[:, 0:NSB * T], ALU.subtract))
            link(V.tensor_copy(tile_rel, rel2))
            count_bad(tmp2, rel2, float(SLOTS), ALU.is_ge)
            count_bad(tmp2, rel2, 0.0, ALU.is_lt, valid=dst2)
            dve.wait_ge(s_raw[1], 48)
            dve.wait_ge(s_slots, 1)
            V.tensor_copy(rawf[:, :, :], raw[:, :, :]).then_inc(s_rawf, 1)
            for c in range(0, CH, 4):
                m = min(4, CH - c)
                dve.wait_ge(s_tabT, (CH + 3) // 4 + c // 4 + 1)
                ins = V.tensor_copy(srci[:, c * P:(c + m) * P], psum[:, c // 4, 0:m * P])
            ins.then_inc(s_srci, 1)
            dve.wait_ge(s_srci, 1)
            link(V.tensor_scalar(src_lo_i, srci[:, 0:NSB * T], P - 1, None, ALU.bitwise_and))
            link(V.tensor_copy(tmp2, src_lo_i))
            link(V.tensor_tensor(key_of, srci[:, 0:NSB * T], tmp2, ALU.subtract))
            link(V.tensor_copy(src_lo, tmp2))
            link(V.scalar_tensor_tensor(key_of, key_of, float(SLOTS) / P, rel2, ALU.mult, ALU.add))
            dve.wait_ge(s_basep, 1)
            link(V.tensor_copy(base_fast[:, :], psum[:, 5, 0:NSB]))
            dst3 = dstf[:, 0:NSB * T].rearrange("p (s t) -> p s t", t=T)
            fast3 = wide(base_fast[:, :].rearrange("p (s t) -> p s t", t=1), 2, T)
            link(V.tensor_tensor(rel[:, :, :], dst3, fast3, ALU.subtract))
            count_bad(tmp2, rel2, float(W), ALU.is_ge)
            count_bad(tmp2, rel2, 0.0, ALU.is_lt, valid=dst2)
            node3 = slot_node[:, :].rearrange("p (c q) -> p c q", q=T)
            link(V.tensor_copy(node3, psum[:, 5, 256:256 + CH * T].rearrange("p (q c) -> p c q", q=T)))
            link(V.tensor_scalar(slot_node[:, :], slot_node[:, :], slot[:, :], None, ALU.add))
            link(V.tensor_copy(slot_abs[:, :], slot_node[:, :]))
            link(V.tensor_copy(slot_abs_i[:, :], slot_node[:, :]))
            block_base = base_fast[:, :].rearrange("p (b two) -> p b two", two=2)[:, 0:NCB, 0]
            link(V.tensor_tensor(slot_node[:, 0:NCB], slot_node[:, 0:NCB], block_base, ALU.subtract))
            count_bad(slot_tmp[:, :], slot_node[:, 0:NCB], float(BW), ALU.is_ge)
            count_bad(slot_tmp[:, :], slot_node[:, 0:NCB], 0.0, ALU.is_lt)
            V.memset(s1[:, :], 0.0).then_inc(s_bad, 1)
            dve.wait_ge(s_badp, 1)
            link(V.tensor_scalar(general[:, :], psum[:, 6, 0:1], 0.5, None, ALU.is_ge))
            link(V.tensor_scalar(fast[:, :], general[:, :], -1.0, 1.0, ALU.mult, ALU.add))
            for t in (slot_node[:, 0:NCB], rel2):
                link(V.tensor_scalar(t, t, 1000.0, fast[:, :], ALU.add, ALU.mult))
                link(V.tensor_scalar(t, t, -1000.0, None, ALU.add))
            link(V.tensor_copy(base_i[:, :], base_fast[0:1, :]))
            V.tensor_scalar(passes_i[:, :], general[0:1, :], float(PASSES - 1), 1.0, ALU.mult, ALU.add).then_inc(s_mode, 1)
            dve.wait_ge(s_mode, 1)
            NBT = NSB * T // BT
            slot_nodes = slot_abs[:, :]
            link(V.tensor_scalar(slot_lo_i[:, :], slot_abs_i[:, :], P - 1, None, ALU.bitwise_and))
            link(V.tensor_copy(slot_lo_f[:, :], slot_lo_i[:, :]))
            link(V.tensor_tensor(slot_nodes, slot_nodes, slot_lo_f[:, :], ALU.subtract))
            link(V.tensor_scalar(slot_hi_b[:, :], slot_nodes, 1.0 / P, None, ALU.mult))
            link(V.tensor_copy(slot_lo_b[:, :], slot_lo_f[:, :]))
            slots3 = wide(iota_bw[:, 0:SLOTS].rearrange("p (t c) -> p t c", t=1), 1, NBT * BT // 2)
            for half in range(2):
                if half:
                    dve.wait_ge(s_slotcnt, 1)
                c0 = half * NBT * BT // 2
                V.tensor_tensor(edge_slot.rearrange("p b (t c) -> p (b t) c", c=SLOTS),
                                wide(tile_rel[:, c0:c0 + NBT * BT // 2].rearrange("p (t c) -> p t c", c=1), 2, SLOTS), slots3,
                                ALU.is_equal).then_inc(s_edgeslot, 1)
            dve.wait_ge(s_slotcnt, 2)
            link(V.memset(slot_cnt[:, :], 0.0))
            link(V.tensor_copy(slot_cnt[:, 0:NBT], psum[:, 6, 128:128 + NBT]))
            passes = dve.value_load(passes_i[0:1, 0:1], min_val=1, max_val=PASSES)
            for g in range(CH):
                k = g % 2
                if g >= 2:
                    dve.wait_ge(s_slothist, g - 1)
                cols = slice(g * T, (g + 1) * T)
                V.tensor_tensor(one_lo[:, k, :, :], digit[:, :, :],
                                wide(slot_lo_b[:, cols].rearrange("p (c t) -> p c t", c=1), 1, P), ALU.is_equal)
                link(V.tensor_tensor(one_hi[:, k, :, :], digit[:, 0:HI, :],
                                     wide(slot_hi_b[:, cols].rearrange("p (c t) -> p c t", c=1), 1, HI), ALU.is_equal))
                V.tensor_tensor(one_hi[:, k, :, :], one_hi[:, k, :, :],
                                wide(slot_cnt[:, cols].rearrange("p (c t) -> p c t", c=1), 1, HI), ALU.mult).then_inc(s_slotoh, 1)
            dve.wait_ge(s_slothist, CH)
            with dve.If(passes > 1):
                with dve.Fori(0, NSB // 2) as i:
                    for k in range(2):
                        dve.wait_ge(s_hfree, 2 * i + k + 1)
                        cols = bass.ds((2 * i + k) * T, T)
                        V.tensor_tensor(one_lo[:, k, :, :], digit[:, :, :],
                                        wide(dlo_b[:, cols].rearrange("p (c t) -> p c t", c=1), 1, P), ALU.is_equal)
                        last = V.tensor_tensor(one_hi[:, k, :, :], digit[:, 0:HI, :],
                                               wide(dhi_b[:, cols].rearrange("p (c t) -> p c t", c=1), 1, HI), ALU.is_equal)
                        last.then_inc(s_oh, 1)
            dve.wait_ge(s_hist, 1)
            link(V.tensor_copy(cnt[:, :], psum[:, 4, 0:NB]))
            V.tensor_scalar(s2[:, :], cnt[:, :], 1.0, None, ALU.add).then_inc(s_deg, 1)
            dve.wait_ge(s_dsq, 1)
            V.reciprocal(dis[:, :], std[:, :]).then_inc(s_dis, 1)
            dve.wait_ge(s_dis, 1)
            dve.wait_ge(s_cntT, 1)
            V.tensor_copy(cntT[:, :], psum[0:NB, 7, 0:P]).then_inc(s_cntTc, 1)

            def bc(t):
                return wide(t[:, :].rearrange("p (b d) -> p b d", d=1), 2, D)

            def layer_norm_relu(n):
                link(V.tensor_reduce(s1[:, :], X[:, :, :], AX, ALU.add))
                link(V.tensor_scalar(mean[:, :], s1[:, :], 1.0 / D, None, ALU.mult))
                link(V.tensor_tensor(Y[:, :, :], X[:, :, :], bc(mean), ALU.subtract))
                link(V.tensor_tensor(Z[:, :, :], Y[:, :, :], Y[:, :, :], ALU.mult))
                V.tensor_reduce(s2[:, :], Z[:, :, :], AX, ALU.add).then_inc(s_var[n], 1)
                dve.wait_ge(s_std[n], 1)
                link(V.reciprocal(rstd[:, :], std[:, :]))
                V.scalar_tensor_tensor(H[:, 1:NB + 1, :], Y[:, :, :], 0.0, bc(rstd), ALU.max, ALU.mult).then_inc(s_hready[n], 1)

            def edge_pass_setup(r, layer):
                link_r(V.tensor_scalar(tmp_e[:, :, 0], base_pass[:, :], general[:, :], None, ALU.mult))
                link_r(V.scalar_tensor_tensor(base[:, :], base_fast[:, :], fast[:, :], tmp_e[:, :, 0], ALU.mult, ALU.add))
                link_r(V.tensor_copy(base_i[:, :], base[0:1, :]))
                link_r(V.tensor_scalar(base_pass[:, :], base_pass[:, :], float(W), None, ALU.add))
                base3 = wide(base[:, :].rearrange("p (s t) -> p s t", t=1), 2, T)
                V.tensor_tensor(rel[:, :, :], dst3, base3, ALU.subtract).then_inc(s_pass[layer], 1)
                dve.wait_ge(s_pass[layer], r + 1)
                dve.sem_inc(s_turn[2], 1)

            s_setup = [None]

            def link_r(ins):
                n, r, s, per = s_setup[0]
                s_setup[0] = (n + 1, r, s, per)
                ins.then_inc(s, 1)
                dve.wait_ge(s, r * per + n + 1)

            def window_onehots(s, out_slot):
                return V.tensor_tensor(out_slot, wide(iota_w.rearrange("p (t c) -> p t c", t=1), 1, T),
                                       wide(rel2[:, bass.ds(s * T, T)].rearrange("p (t c) -> p t c", c=1), 2, W), ALU.is_equal)

            dve.wait_ge(s_x, 32)
            layer_norm_relu(0)
            for c in range(0, NB, 4):
                m = min(4, NB - c)
                dve.wait_ge(s_tr, c // 4 + 1)
                V.tensor_copy(hT[0:D, c * P:(c + m) * P], psum[0:D, (c // 4) % 2, 0:m * P]).then_inc(s_trc, 1)
            for c in range(0, NB, T):
                m = min(T, NB - c)
                dve.wait_ge(s_mm, c // T + 1)
                g3 = wide(dis[:, c:c + m].rearrange("p (b d) -> p b d", d=1), 2, D)
                V.tensor_tensor(Y[:, c:c + m, :], psum[:, 2 + (c // T) % 2, 0:m * D].rearrange("p (b d) -> p b d", d=D), g3,
                                ALU.mult).then_inc(s_mmc, 1)

            dve.wait_ge(s_mmc, (NB + T - 1) // T)
            link(V.tensor_copy(gtab[:, :, 0, :], Y[:, :, :]))
            link(V.tensor_tensor(Z[:, :, :], Y[:, :, :], gtab[:, :, 0, :], ALU.subtract))
            link(V.tensor_copy(gtab[:, :, 1, :], Z[:, :, :]))
            link(V.tensor_tensor(Z[:, :, :], Z[:, :, :], gtab[:, :, 1, :], ALU.subtract))
            V.tensor_copy(gtab[:, :, 2, :], Z[:, :, :]).then_inc(s_gtab, 1)
            dve.wait_ge(s_gtab, 1)
            passes = dve.value_load(passes_i[0:1, 0:1], min_val=1, max_val=PASSES)

            def count_onehots(i, j, g):
                tile = i * MB * BT + j * BT + g * T
                dve.wait_ge(counted, tile + T)
                V.tensor_tensor(one_lo[:, g, :, :], digit[:, :, :],
                                wide(src_lo[:, bass.ds(tile, T)].rearrange("p (c t) -> p c t", c=1), 1, P), ALU.is_equal)
                for t in range(T):
                    V.tensor_scalar(keys[:, g * T + t, :], key_digit[:, :], key_of[:, bass.ds(tile + t, 1)], None,
                                    ALU.is_equal).then_inc(key_ready, 1)

            def slot_sums(i, j):
                V.tensor_scalar(slot_oh[:, j % 2, :], iota_bw[:, :], slot_node[:, bass.ds(i * MB + j - 2, 1)], None, ALU.is_equal)
                dve.wait_ge(multiplied, i * MB + j + 1)
                V.tensor_reduce(part[:, j % 2, :], psum[:, 4 + j % 2, 0:NPART * D].rearrange("p (k d) -> p d k", d=D), AX,
                                ALU.add).then_inc(part_ready, 1)

            def add_counted(i, j, b0, place_):
                dve.wait_ge(placed, i * MB + j - 1)
                dve.wait_ge(acc_add[0], i * ADDS + place_ + 1)
                V.tensor_tensor(acc[0:D, bass.ds(b0, BW)], acc[0:D, bass.ds(b0, BW)], psum[0:D, 6, 0:BW],
                                ALU.add).then_inc(acc_add[0], 1)

            def mixed_step(i, j):
                started = not isinstance(i, int) or i * MB + j >= 2
                if started:
                    b0 = dve.value_load(base_i[0:1, bass.ds((i * MB + j - 2) * 2, 1)], min_val=0, max_val=NP - BW)
                if 1 <= j <= MS:
                    g0 = dve.value_load(base_i[0:1, bass.ds(i * MS + j - 1 + S0, 1)], min_val=0, max_val=NP - W)
                if j < MS:
                    dve.wait_ge(summed[0], i * MS + j + 1)
                    window_onehots(i * MS + j + S0, onehot0[:, j % U]).then_inc(onehot[0], 1)
                count_onehots(i, j, 0)
                if started:
                    slot_sums(i, j)
                count_onehots(i, j, 1)
                if 1 <= j <= MS:
                    dve.wait_ge(summed[0], i * MS + j - 1 + U + 1)
                    dve.wait_ge(acc_add[0], i * ADDS + place_gathered(j - 1) + 1)
                    V.tensor_tensor(acc[0:D, bass.ds(g0, W)], acc[0:D, bass.ds(g0, W)], psum[0:D, 7, 0:W],
                                    ALU.add).then_inc(acc_add[0], 1)
                if started:
                    add_counted(i, j, b0, place_counted(j))
                else:
                    dve.wait_ge(acc_add[0], place_counted(j) + 1)
                    dve.sem_inc(acc_add[0], 1)

            mixed_bodies(dve, mixed_step)
            for j in range(2):
                b0 = dve.value_load(base_i[0:1, (NCB + j - 2) * 2:(NCB + j - 2) * 2 + 1], min_val=0, max_val=NP - BW)
                slot_sums(NMIX, j)
                add_counted(NMIX, j, b0, j)
            dve.wait_ge(acc_add[0], NMIX * ADDS + 3)

            def edge_passes(layer):
                with dve.Fori(0, passes) as r:
                    s_setup[0] = (0, r, s_pdone[layer], 4)
                    edge_pass_setup(r, layer)

                    def onehots_of(i, k):
                        n = r * NSB + i * U + k
                        dve.wait_ge(summed[layer], n + 1)
                        out_slot = eo[:, k, :, D:2 * D] if layer == 1 else onehot0[:, k]
                        window_onehots(i * U + k, out_slot).then_inc(onehot[layer], 1)

                    def add_rows(i, k):
                        dve.wait_ge(gathered[1][k], 16 * T * (i + 1))
                        dve.wait_ge(pre_done, r * NSB + i * U + k + 1)
                        V.tensor_tensor(msg[:, k % 2, :, :], psum[:, 4 + k % 2, :].rearrange("p (t d) -> p t d", d=D),
                                        rows[:, k, :, :], ALU.add).then_inc(added, 1)

                    def add_sums(i, k, b0):
                        n = r * NSB + i * U + k
                        dve.wait_ge(acc_add[layer], n + 2)
                        dve.wait_ge(summed[layer], n + U + 1)
                        V.tensor_tensor(acc[0:D, bass.ds(b0, W)], acc[0:D, bass.ds(b0, W)], psum[0:D, 6 + k % 2, 0:W],
                                        ALU.add).then_inc(acc_add[layer], 1)

                    def step(i, k, last):
                        b0 = dve.value_load(base_i[0:1, bass.ds(i * U + k, 1)], min_val=0, max_val=NP - W)
                        if not last or k + 3 < U:
                            onehots_of(*ahead(i, k, 3))
                        if layer == 1:
                            add_rows(i, k)
                        add_sums(i, k, b0)

                    if layer == 1:
                        dve.wait_ge(counts_reset[1], r + 1)
                        dve.sem_inc(s_turn[2], 1)
                    for k in range(3):
                        onehots_of(0, k)
                    for_superblocks(dve, step)
                dve.wait_ge(acc_add[layer], passes * NSB + 2)
                dve.sem_inc(s_turn[2], 1)

            with dve.If(passes > 1):
                edge_passes(2)
            link(V.memset(base_pass[:, :], 0.0))
            V.memset(s1[:, :], 0.0).then_inc(s_stc, 1)
            for c in range(0, NB, T):
                m = min(T, NB - c)
                dve.wait_ge(s_stT, c // T + 1)
                V.tensor_tensor(Z[:, c:c + m, :], psum[:, (c // T) % 2, 0:m * D].rearrange("p (b d) -> p b d", d=D),
                                Y[:, c:c + m, :], ALU.add).then_inc(s_stc, 1)
            link(V.tensor_tensor(X[:, :, :], X[:, :, :], H[:, 1:NB + 1, :], ALU.add))
            dve.wait_ge(s_stc, (NB + T - 1) // T + 1)
            link(V.tensor_tensor(Z[:, :, :], Z[:, :, :], bc(dis), ALU.mult))
            dve.wait_ge(s_wt, 11 * 16)
            b3 = wide(b_l0[:, :].rearrange("p (b d) -> p b d", b=1), 1, NB)
            V.tensor_tensor(Z[:, :, :], Z[:, :, :], b3, ALU.add).then_inc(s_gelu_in, 1)
            dve.wait_ge(s_gelu, 1)
            link(V.tensor_tensor(X[:, :, :], X[:, :, :], Z[:, :, :], ALU.add))
            layer_norm_relu(1)
            for c in range(0, NB, 4):
                m = min(4, NB - c)
                dve.wait_ge(s_tr, (NB + 3) // 4 + c // 4 + 1)
                V.tensor_copy(hT[D:2 * D, c * P:(c + m) * P], psum[D:2 * D, (c // 4) % 2, 0:m * P]).then_inc(s_trc, 1)
            for c in range(0, NB, T):
                m = min(T, NB - c)
                dve.wait_ge(s_mm, (NB + T - 1) // T + c // T + 1)
                j = 2 + 2 * ((c // T) % 2)
                ps3 = psum[:, j:j + 2, :].rearrange("p a (b d) -> p (a b) d", d=2 * D)[:, 0:m, :]
                V.tensor_copy(Y[:, c:c + m, :], ps3[:, :, 0:D])
                b1 = wide(b_msg1[:, :].rearrange("p (b d) -> p b d", b=1), 1, m)
                V.tensor_tensor(Z[:, c:c + m, :], ps3[:, :, D:2 * D], b1, ALU.add).then_inc(s_mmc, 1)
            link(V.memset(acc[0:D, :], 0.0))
            edge_passes(1)
            V.memset(s1[:, :], 0.0).then_inc(s_aclr, 1)
            for c in range(0, NP, 512):
                m = min(512, NP - c)
                q = c // 512
                dve.wait_ge(s_u1, q + 1)
                V.tensor_copy(hT[0:D, c:c + m], psum[0:D, q % 2, 0:m]).then_inc(s_u1c, 1)
            dve.wait_ge(s_u1, NP // 512 + 1)
            V.memset(acc[D:D + 1, :], 1.0).then_inc(s_one_row, 1)
            for c in range(0, NB, T):
                m = min(T, NB - c)
                dve.wait_ge(s_u3, c // T + 1)
                V.tensor_tensor(Y[:, c:c + m, :], psum[:, 4 + (c // T) % 2, 0:m * D].rearrange("p (b d) -> p b d", d=D),
                                X[:, c:c + m, :], ALU.add).then_inc(s_u3c, 1)

        @block.scalar
        def _(act):
            act.wait_ge(s_const, 12)

            def sqrt_var(n):
                act.wait_ge(s_var[n], 1)
                nc.scalar.activation(std[:, :], s2[:, :], ACT.Sqrt, bias=eps_t[:, :], scale=1.0 / D).then_inc(s_std[n], 1)

            act.wait_ge(s_deg, 1)
            nc.scalar.activation(std[:, :], s2[:, :], ACT.Sqrt).then_inc(s_dsq, 1)
            sqrt_var(0)

            def evacuate(i, j):
                act.wait_ge(multiplied, i * MB + j + 1)
                for t in range(BT):
                    act.wait_ge(counted, i * MB * BT + j * BT + t + 1 + BT)
                    nc.scalar.activation(counts[:, j % 2, :, t * SLOTS:(t + 1) * SLOTS],
                                         psum[:, t % 4, 0:KEYS].rearrange("p (h m) -> p h m", m=SLOTS), ACT.Copy
                                         ).then_inc(evacuated, 1)

            mixed_bodies(act, evacuate)
            act.wait_ge(s_gelu_in, 1)
            nc.scalar.activation(Z[:, :, :], Z[:, :, :], ACT.Gelu).then_inc(s_gelu, 1)
            sqrt_var(1)
            passes = act.value_load(passes_i[0:1, 0:1], min_val=1, max_val=PASSES)
            with act.Fori(0, passes) as r:
                def copy_transposed(i, k, older):
                    n = r * NSB + i * U + k
                    if older:
                        act.wait_ge(pre_done, n - 1)
                    act.wait_ge(transposed, n + 1)
                    nc.scalar.activation(eoT[:, k % 2, :, :],
                                         psum[:, 2 * (k % 2):2 * (k % 2) + 2, :].rearrange("p a (t e) -> p (a t) e", e=P),
                                         ACT.Copy).then_inc(eoT_ready, 1)

                def relu(i, k):
                    act.wait_ge(added, r * NSB + i * U + k + 1 + U)
                    nc.scalar.activation(msg[:, k % 2, :, :], msg[:, k % 2, :, :], ACT.Relu).then_inc(relu_done, 1)

                def step(i, k, last):
                    if not last or k + 2 < U:
                        copy_transposed(*ahead(i, k, 2), True)
                    relu(i, k)

                copy_transposed(0, 0, False)
                copy_transposed(0, 1, False)
                for_superblocks(act, step)
            act.wait_ge(s_wt, 11 * 16)
            for c in range(0, NP, 512):
                m = min(512, NP - c)
                q = c // 512
                act.wait_ge(s_u2, q + 1)
                nc.scalar.activation(acc[0:D, c:c + m], psum[0:D, 2 + q % 2, 0:m], ACT.Relu, bias=b_upd1[:, :]).then_inc(s_u2c, 1)

        @block.tensor
        def _(pe):
            TT = nc.tensor
            pe.wait_ge(s_const, 12)

            def index_transposes(n):
                pe.wait_ge(s_rawf, n + 1)
                for c in range(CH):
                    ins = TT.transpose(psum[:, c // 4, (c % 4) * P:(c % 4 + 1) * P], rawf[:, c, :], ident[:, :])
                    if c % 4 == 3 or c == CH - 1:
                        ins.then_inc(s_tabT, 1)

            index_transposes(0)
            pe.wait_ge(s_dst_ready, 1)
            for c in range(0, NSB * T, 512):
                m = min(512, NSB * T - c)
                ins = TT.matmul(psum[:, c // 512, 0:m], first_row[:, :], dstf[:, c:c + m], start=True, stop=True)
            ins.then_inc(s_tile0, 1)
            TT.matmul(psum[:, 5, 0:NSB], first_row[:, :], dstf[:, 0:NSB * T:T], start=True, stop=True).then_inc(s_basep, 1)
            for q in range(T):
                ins = TT.matmul(psum[:, 5, 256 + q * CH:256 + (q + 1) * CH], expand[:, q, :], rawf[:, :, 0], start=True, stop=True)
            ins.then_inc(s_slots, 1)
            index_transposes(1)
            pe.wait_ge(s_bad, 1)
            TT.matmul(psum[:, 6, 0:1], ones[:, :], bad[:, :], start=True, stop=True).then_inc(s_badp, 1)
            pe.wait_ge(s_mode, 1)
            passes = pe.value_load(passes_i[0:1, 0:1], min_val=1, max_val=PASSES)
            NHALF = NSB * T // BT // 2
            for half in range(2):
                pe.wait_ge(s_edgeslot, half + 1)
                for b in range(NHALF):
                    col = 128 + half * NHALF + b
                    ins = TT.matmul(psum[:, 6, col:col + 1], edge_slot[:, b, :], ones_b[:, :], start=True, stop=True)
                ins.then_inc(s_slotcnt, 1)
            for g in range(CH):
                pe.wait_ge(s_slotoh, g + 1)
                for t in range(T):
                    ins = TT.matmul(psum[:, 4, 0:HI], one_lo[:, g % 2, :, t], one_hi[:, g % 2, :, t],
                                    start=(g + t == 0), stop=(g + t == CH + T - 2))
                ins.then_inc(s_slothist, 1)
            with pe.If(passes > 1):
                TT.matmul(psum[:, 4, 0:HI], zeros[:, :], zeros[:, 0:HI], start=True, stop=False)
                pe.sem_inc(s_hfree, 2)
                with pe.Fori(0, NSB // 2) as i:
                    for k in range(2):
                        pe.wait_ge(s_oh, 2 * i + k + 1)
                        for t in range(T):
                            ins = TT.matmul(psum[:, 4, 0:HI], one_lo[:, k, :, t], one_hi[:, k, :, t], start=False, stop=False)
                        ins.then_inc(s_hfree, 1)
                TT.matmul(psum[:, 4, 0:HI], zeros[:, :], zeros[:, 0:HI], start=False, stop=True)
            TT.matmul(psum[:, 7, 0:1], ones[:, :], bad[:, :], start=True, stop=True).then_inc(s_hist, 1)
            pe.wait_ge(s_dis, 1)
            TT.transpose(psum[0:NB, 7, 0:P], cnt[:, :], ident[:, :]).then_inc(s_cntT, 1)

            pe.wait_ge(s_hready[0], 1)
            pe.wait_ge(s_srci, 1)
            for b in range(NB):
                c = b // 4
                if b % 4 == 0 and c >= 2:
                    pe.wait_ge(s_trc, c - 1)
                ins = TT.transpose(psum[0:D, c % 2, (b % 4) * P:(b % 4 + 1) * P], H[:, b + 1, :], ident[:, :])
                if b % 4 == 3 or b == NB - 1:
                    ins.then_inc(s_tr, 1)
            pe.wait_ge(s_wt, 11 * 16)
            pe.wait_ge(s_trc, (NB + 3) // 4)
            for b in range(NB):
                c = b // T
                if b % T == 0 and c >= 2:
                    pe.wait_ge(s_mmc, c - 1)
                ins = TT.matmul(psum[:, 2 + c % 2, (b % T) * D:(b % T + 1) * D], hT[0:D, b * P:(b + 1) * P], w_l0[:, :],
                                start=True, stop=True)
                if b % T == T - 1 or b == NB - 1:
                    ins.then_inc(s_mm, 1)

            passes = pe.value_load(passes_i[0:1, 0:1], min_val=1, max_val=PASSES)
            pe.wait_ge(s_mmc, (NB + T - 1) // T)
            pe.wait_ge(s_acc0, 1)
            pe.wait_ge(s_gtab, 1)
            for credited, n in ((counted, BT), (evacuated, 4), (multiplied, 2), (part_ready, 2), (summed[0], U), (acc_add[0], 1)):
                pe.sem_inc(credited, n)

            def multiply(i, j, q, of):
                if q == 0:
                    pe.wait_ge(evacuated, (i * MB + j) * BT + 4)
                    pe.wait_ge(part_ready, i * MB + j)
                for h in range(q * HS // of, (q + 1) * HS // of):
                    ins = TT.matmul(psum[:, 4 + (j + 1) % 2, 0:NPART * D], counts[:, (j + 1) % 2, h, :],
                                    gtab[:, h, :, :].rearrange("p k d -> p (k d)"), start=(h == 0), stop=(h == HS - 1))
                if q == of - 1:
                    ins.then_inc(multiplied, 1)

            def place(i, j):
                pe.wait_ge(part_ready, i * MB + j + 1)
                if not isinstance(i, int) or i * MB + j >= 3:
                    pe.wait_ge(acc_add[0], i * ADDS + (place_counted(j - 1) + 2 if j else 1))
                TT.matmul(psum[0:D, 6, 0:BW], part[:, j % 2, :], slot_oh[:, j % 2, :], start=True, stop=True).then_inc(placed, 1)

            def sum_gathered(i, k):
                pe.wait_ge(onehot[0], i * MS + k + 1)
                pe.wait_ge(gathered[0][k % U], 16 * T * (i * (MS // U) + k // U + 1))
                if k >= 1:
                    pe.wait_ge(acc_add[0], i * ADDS + place_gathered(k - 1) + 2)
                elif not isinstance(i, int):
                    pe.wait_ge(acc_add[0], i * ADDS + (place_gathered(MS - 1) + 2 - ADDS))
                for t in range(T):
                    ins = TT.matmul(psum[0:D, 7, 0:W], rows[:, k % U, t, :], onehot0[:, k % U, t, :],
                                    start=(t == 0), stop=(t == T - 1))
                ins.then_inc(summed[0], 1)

            def mixed_step(i, j):
                first = isinstance(i, int) and i * MB + j
                for t in range(BT):
                    tile = i * MB * BT + j * BT + t
                    pe.wait_ge(key_ready, tile + 1)
                    pe.wait_ge(evacuated, tile + 1)
                    TT.matmul(psum[:, t % 4, 0:KEYS], one_lo[:, t // T, :, t % T], keys[:, t, :],
                              start=True, stop=True).then_inc(counted, 1)
                    if t >= 2 and (not isinstance(i, int) or first >= 1):
                        multiply(i, j, t - 2, BT - 2)
                    if t == 4 and (not isinstance(i, int) or first >= 2):
                        place(i, j)
                if j < MS:
                    sum_gathered(i, j)

            mixed_bodies(pe, mixed_step)
            multiply(NMIX, 0, 0, 1)
            place(NMIX, 0)
            place(NMIX, 1)

            with pe.If(passes > 1):
                pe.sem_inc(summed[2], U)
                pe.sem_inc(acc_add[2], 2)
                with pe.Fori(0, passes) as r:
                    pe.wait_ge(counts_reset[2], r + 1)
                    pe.sem_inc(s_turn[3], 1)
                    with pe.Fori(0, NIT) as i:
                        for k in range(U):
                            n = r * NSB + i * U + k
                            pe.wait_ge(onehot[2], n + 1)
                            pe.wait_ge(gathered[2][k], 16 * T * (i + 1))
                            pe.wait_ge(acc_add[2], n + 1)
                            for t in range(T):
                                ins = TT.matmul(psum[0:D, 6 + k % 2, 0:W], rows[:, k, t, :], onehot0[:, k, t, :],
                                                start=(t == 0), stop=(t == T - 1))
                            ins.then_inc(summed[2], 1)
            pe.wait_ge(s_stc, 1)
            for b in range(NB):
                c = b // T
                if b % T == 0 and c >= 2:
                    pe.wait_ge(s_stc, c)
                ins = TT.transpose(psum[:, c % 2, (b % T) * D:(b % T + 1) * D], acc[0:D, b * P:(b + 1) * P], ident[0:D, 0:D])
                if b % T == T - 1 or b == NB - 1:
                    ins.then_inc(s_stT, 1)
            pe.wait_ge(s_hready[1], 1)
            for b in range(NB):
                c = b // 4
                if b % 4 == 0 and c >= 2:
                    pe.wait_ge(s_trc, (NB + 3) // 4 + c - 1)
                ins = TT.transpose(psum[:, c % 2, (b % 4) * P:(b % 4 + 1) * P],
                                   H[:, b:b + 2, :].rearrange("p b d -> p (b d)"), ident[:, :])
                if b % 4 == 3 or b == NB - 1:
                    ins.then_inc(s_tr, 1)
            pe.wait_ge(s_trc, 2 * ((NB + 3) // 4))
            for b in range(NB):
                c = b // T
                if b % T == 0 and c >= 2:
                    pe.wait_ge(s_mmc, (NB + T - 1) // T + c - 1)
                j = 2 + 2 * (c % 2) + (b % T) // 4
                ins = TT.matmul(psum[:, j, (b % 4) * 2 * D:(b % 4 + 1) * 2 * D], hT[D:2 * D, b * P:(b + 1) * P], w_ab[D:2 * D, :],
                                start=True, stop=True)
                if b % T == T - 1 or b == NB - 1:
                    ins.then_inc(s_mm, 1)
            pe.wait_ge(s_mmc, 2 * ((NB + T - 1) // T))
            pe.wait_ge(s_wc, 16 * U)
            pe.sem_inc(summed[1], U)
            pe.sem_inc(added, U)
            pe.sem_inc(acc_add[1], 2)
            with pe.Fori(0, passes) as r:
                def transpose_edges(i, k):
                    pe.wait_ge(onehot[1], r * NSB + i * U + k + 1)
                    pe.wait_ge(e_in[k], 32 * (r * NIT + i + 1))
                    for t in range(T):
                        ins = TT.transpose(psum[:, 2 * (k % 2) + t // 4, (t % 4) * P:(t % 4 + 1) * P], eo[:, k, t, :], ident[:, :])
                    ins.then_inc(transposed, 1)

                def edge_and_target_terms(i, k):
                    pe.wait_ge(eoT_ready, r * NSB + i * U + k + 1)
                    pe.wait_ge(b_in[k], 16 * (r * NIT + i + 1))
                    for t in range(T):
                        ins = TT.matmul(psum[:, 4 + k % 2, t * D:(t + 1) * D], eoT[:, k % 2, t, :], wb[:, k, :],
                                        start=True, stop=True)
                    ins.then_inc(pre_done, 1)

                def sum_messages(i, k):
                    n = r * NSB + i * U + k
                    pe.wait_ge(relu_done, n + 1)
                    pe.wait_ge(acc_add[1], n + 1)
                    for t in range(T):
                        ins = TT.matmul(psum[0:D, 6 + k % 2, 0:W], msg[:, k % 2, t, :], eo[:, k, t, D:2 * D],
                                        start=(t == 0), stop=(t == T - 1))
                    ins.then_inc(summed[1], 1)

                def step(i, k, last):
                    if not last or k + 2 < U:
                        transpose_edges(*ahead(i, k, 2))
                    if not last or k + 1 < U:
                        edge_and_target_terms(*ahead(i, k, 1))
                    sum_messages(i, k)

                transpose_edges(0, 0)
                transpose_edges(0, 1)
                edge_and_target_terms(0, 0)
                for_superblocks(pe, step)
            pe.wait_ge(s_aclr, 1)
            pe.wait_ge(s_cntr, 16)
            for c in range(0, NP, 512):
                m = min(512, NP - c)
                q = c // 512
                if q >= 2:
                    pe.wait_ge(s_u1c, q - 1)
                TT.matmul(psum[0:D, q % 2, 0:m], w_msg2[:, :], acc[:, c:c + m], start=True, stop=True).then_inc(s_u1, 1)
            for c in range(0, NP, 512):
                m = min(512, NP - c)
                q = c // 512
                pe.wait_ge(s_u1c, q + 1)
                if q >= 2:
                    pe.wait_ge(s_u2c, q - 1)
                TT.matmul(psum[0:D, 2 + q % 2, 0:m], w_upd1[:, :], hT[:, c:c + m], start=True, stop=True).then_inc(s_u2, 1)
            pe.wait_ge(s_u2c, NP // 512 + 1)
            pe.wait_ge(s_one_row, 1)
            for b in range(NB):
                c = b // T
                if b % T == 0 and c >= 2:
                    pe.wait_ge(s_u3c, c - 1)
                ins = TT.matmul(psum[:, 4 + c % 2, (b % T) * D:(b % T + 1) * D], acc[:, b * P:(b + 1) * P], w_upd2[:, :],
                                start=True, stop=True)
                if b % T == T - 1 or b == NB - 1:
                    ins.then_inc(s_u3, 1)


_INS = ['x', 'src', 'dst', 'edge_attr_64', 'L0_gnn_W', 'L0_gnn_b', 'L1_gnn_msg_W1', 'L1_gnn_msg_b1', 'L1_gnn_msg_W2',
        'L1_gnn_msg_b2', 'L1_gnn_upd_W1', 'L1_gnn_upd_b1', 'L1_gnn_upd_W2', 'L1_gnn_upd_b2']


def kernel(**inputs):
    import numpy as _np
    import concourse.bacc as _bacc
    from concourse import mybir as _mybir
    from concourse.bass_utils import run_bass_kernel_spmd as _run

    nc = _bacc.Bacc("TRN2", target_bir_lowering=False, num_devices=1)
    arrays, args = {}, []
    for name in _INS:
        a = _np.ascontiguousarray(inputs[name])
        arrays[f"in_{name}_dram"] = a
        args.append(nc.dram_tensor(f"in_{name}_dram", a.shape, _mybir.dt.from_np(a.dtype), kind="ExternalInput").ap())
    args.append(nc.dram_tensor("out_0_dram", inputs['x'].shape, _mybir.dt.float32, kind="ExternalOutput").ap())
    gnn_two_layers(nc, *args)
    r = _run(nc, [arrays], core_ids=[0])
    return r.results[0]["out_0_dram"]
```
